# Optimizing a Trainium2 kernel written in Bass

```python
import numpy as np
import jax
import jax.numpy as jnp

def _softmax(x, axis=-1):
    return jax.nn.softmax(x, axis=axis)

def _gelu(x):
    return jax.nn.gelu(x, approximate=True)

def _silu(x):
    return jax.nn.silu(x)

def _sigmoid(x):
    return jax.nn.sigmoid(x)

def _layernorm(x, axis=-1, eps=1e-05):
    m = jnp.mean(x, axis=axis, keepdims=True)
    v = jnp.var(x, axis=axis, keepdims=True)
    return (x - m) / jnp.sqrt(v + eps)

def _scatter_add(tgt, idx, src, axis=0):
    return tgt.at[idx].add(src)

def _segment_sum(src, seg, n):
    return jax.ops.segment_sum(src, seg, n)
kernel_name = 'mk_gnn_resnorm_d1_gnn_r8_6ab0a4'

def setup_inputs(seed: int=0):
    np.random.seed(seed)
    _w = jnp.asarray

    def _rec_inputs():
        import jax
        import jax.numpy as jnp
        _gk = jax.random.key(seed)
        x = -0.0005121 + 1.001 * jax.random.normal(jax.random.fold_in(_gk, 1), (6250, 64), jnp.float32)
        src = jax.random.randint(jax.random.fold_in(_gk, 2), (200000,), 0, 6250, jnp.int32)
        dst = jax.random.randint(jax.random.fold_in(_gk, 3), (200000,), 0, 6250, jnp.int32)
        _o = jnp.argsort(dst, stable=True)
        src = src[_o]
        dst = dst[_o]
        return (x, src, dst)
    x, src, dst = _rec_inputs()

    def _L0_gnn_setup():
        import jax, jax.numpy as jnp
        import numpy as np
        N_NODES = 6250
        N_EDGES = 100000
        IN_CH = 64
        HID = 128
        OUT_CH = 64
        BN_EPS = 1e-05
        key = jax.random.key(seed)
        k = jax.random.split(key, 6)
        x = jax.random.normal(k[0], (N_NODES, IN_CH), dtype=jnp.float32)
        edge_index = jax.random.randint(k[1], (2, N_EDGES), 0, N_NODES, dtype=jnp.int64)
        gamma = jnp.ones((IN_CH,), dtype=jnp.float32)
        beta = jnp.zeros((IN_CH,), dtype=jnp.float32)
        W1 = jax.random.normal(k[2], (2 * IN_CH, HID), dtype=jnp.float32) * 0.05
        b1 = jnp.zeros((HID,), dtype=jnp.float32)
        W2 = jax.random.normal(k[3], (HID, OUT_CH), dtype=jnp.float32) * 0.05
        b2 = jnp.zeros((OUT_CH,), dtype=jnp.float32)
        return {'x': x, 'edge_index': edge_index, 'gamma': gamma, 'beta': beta, 'W1': W1, 'b1': b1, 'W2': W2, 'b2': b2}
    _L0_gnn_all = _L0_gnn_setup()
    _L0_gnn_in = {k: v for k, v in _L0_gnn_all.items() if k in ('gamma', 'beta', 'W1', 'b1', 'W2', 'b2')}
    del _L0_gnn_all
    return {'x': x, 'src': src, 'dst': dst, 'L0_gnn_gamma': _L0_gnn_in['gamma'], 'L0_gnn_beta': _L0_gnn_in['beta'], 'L0_gnn_W1': _L0_gnn_in['W1'], 'L0_gnn_b1': _L0_gnn_in['b1'], 'L0_gnn_W2': _L0_gnn_in['W2'], 'L0_gnn_b2': _L0_gnn_in['b2']}

def reference(x, src, dst, L0_gnn_gamma, L0_gnn_beta, L0_gnn_W1, L0_gnn_b1, L0_gnn_W2, L0_gnn_b2):
    import jax
    import jax.numpy as jnp

    def _L0_gnn_ref(x, edge_index, gamma, beta, W1, b1, W2, b2):
        import jax, jax.numpy as jnp
        import numpy as np
        N_NODES = 6250
        N_EDGES = 100000
        IN_CH = 64
        HID = 128
        OUT_CH = 64
        BN_EPS = 1e-05
        mean = jnp.mean(x, axis=0)
        var = jnp.mean(jnp.square(x - mean), axis=0)
        xn = (x - mean) * jax.lax.rsqrt(var + BN_EPS) * gamma + beta
        src = edge_index[0]
        dst = edge_index[1]
        xi = xn[dst]
        xj = xn[src]
        feat = jnp.concatenate([xi, xj - xi], axis=-1)
        h = jax.nn.relu(feat @ W1 + b1)
        msg = h @ W2 + b2
        agg = jax.ops.segment_max(msg, dst, num_segments=N_NODES)
        agg = jnp.where(jnp.isfinite(agg), agg, 0.0)
        return jax.nn.relu(agg)
    edge_index = jnp.stack([src, dst])
    x = _layernorm(x + _L0_gnn_ref(x, edge_index, L0_gnn_gamma, L0_gnn_beta, L0_gnn_W1, L0_gnn_b1, L0_gnn_W2, L0_gnn_b2), axis=-1)
    return x

_drawn_inputs = setup_inputs


def setup_inputs(seed=0):
    import zlib

    import numpy as np

    out = dict(_drawn_inputs(seed))
    spreads = {'L0_gnn_gamma': (1.0, 0.2),
     'L0_gnn_beta': (0.0, 0.504),
     'L0_gnn_b1': (0.0, 0.1),
     'L0_gnn_b2': (0.0, 0.1)}
    factors = {}
    for name, (base, spread) in spreads.items():
        noise = np.random.default_rng([zlib.crc32(name.encode()), seed]).standard_normal(out[name].shape)
        drawn = base * np.exp(spread * noise) if base else spread * noise
        out[name] = jnp.asarray(drawn.astype(out[name].dtype))
    for name, factor in factors.items():
        out[name] = (out[name] * factor).astype(out[name].dtype)
    return out
```

```python
import concourse.bass as bass
import concourse.mybir as mybir
import numpy as np
from contextlib import ExitStack


def edge_conv_program(nc, x, src, dst, gamma, beta, W1, b1, W2, b2, out):
    f32, i32 = mybir.dt.float32, mybir.dt.int32
    ALU, ACT, AX = mybir.AluOpType, mybir.ActivationFunctionType, mybir.AxisListType

    P = 128
    N, C = x.shape
    E = src.shape[0]
    HID = W1.shape[1]
    TG = 4
    GE = TG * P
    SG = 7
    SE = SG * GE
    NSB = -(-E // (2 * SE)) * 2
    ITERS, IG = NSB // 2, 2 * SG
    EP = NSB * SE
    EC = EP // P
    TILES = EP // P
    GT = -(-E // P)
    TB = -(-TILES // P)
    FULL_T = E // P
    REST = E - FULL_T * P
    NB = -(-N // P)
    NP = NB * P
    NLAST = N - (P - 1) * NB
    ELAST = E - (P - 1) * EC
    WIDE = 112
    SCALE = -(2.0 ** 112)
    EPS = 1e-5
    CREDIT_ST, CREDIT_DMA, CREDIT_CUM = 2, 16, 1
    assert 0 < NLAST <= NB and 0 < ELAST <= EC and TB * P >= TILES

    x_pad = nc.dram_tensor("x_pad", [NP + P, C], f32, kind="Internal").ap()
    keys_dram = nc.dram_tensor("keys_dram", [EP + 1], f32, kind="Internal").ap()
    run_dram = nc.dram_tensor("run_dram", [EP, C], f32, kind="Internal").ap()
    dst_dram = nc.dram_tensor("dst_dram", [EP], i32, kind="Internal").ap()
    ends_dram = nc.dram_tensor("ends_dram", [NP + P + 1], i32, kind="Internal").ap()

    ctx = ExitStack()
    with ctx:
        def sb(name, shape, dt=f32):
            return ctx.enter_context(nc.sbuf_tensor(name, shape, dt))

        def pb(name, shape, dt=f32):
            return ctx.enter_context(nc.psum_tensor(name, shape, dt))

        def sem(name):
            return ctx.enter_context(nc.semaphore(name))

        ident = sb("ident", [P, P])
        tri = sb("tri", [P, P])
        ones = sb("ones", [P, P])
        slot_col = sb("slot_col", [P, 1])
        sb_base = sb("sb_base", [P, NSB])
        zeros = sb("zeros", [P, C])
        zeros_i = sb("zeros_i", [P, NB + 3], i32)
        front_key = sb("front_key", [1, 1])
        src_t = sb("src_t", [P, TB, P], i32)
        src_f = sb("src_f", [P, TB, P])
        src_ix = sb("src_ix", [P, TB * P], i32)
        dst_r = sb("dst_r", [P, EC + 1], i32)
        keys = sb("keys", [P, EC])
        step = sb("step", [P, EC])
        win0 = sb("win0", [P, NSB + 1], i32)
        win_step = sb("win_step", [P, NSB])
        win_key = sb("win_key", [P, NSB])
        order_col = sb("order_col", [P, 4])
        order_min = sb("order_min", [1, 1])
        in_order = sb("in_order", [1, 1], i32)
        xn = sb("xn", [P, NB, C])
        xc = sb("xc", [P, NB, C])
        mean_b = sb("mean_b", [P, C])
        w_raw = sb("w_raw", [P, HID])
        w_a = sb("w_a", [P, HID])
        w_cat = sb("w_cat", [P, HID])
        w2 = sb("w2", [HID, C])
        b1c = sb("b1c", [HID, 1])
        bias1 = sb("bias1", [HID, 1])
        b2b = sb("b2b", [P, C])
        gam = sb("gam", [P, 1])
        bet = sb("bet", [P, 1])
        bn = sb("bn", [P, 6])
        ix = [sb(f"ix{u}", [P, SG * TG], i32) for u in range(2)]
        xs = sb("xs", [P, IG, TG, C])
        kb2 = sb("kb2", [P, 2 * (SE + 1)])
        kb = [kb2[:, u * (SE + 1):(u + 1) * (SE + 1)] for u in range(2)]
        xwin = [sb(f"xwin{u}", [P, C]) for u in range(2)]
        onehot = sb("onehot", [P, 2, GE])
        cnt = sb("cnt", [P, 2, SG])
        cnt2 = sb("cnt2", [P, 2])
        cum_i = sb("cum_i", [P, 2], i32)
        reset = sb("reset", [C, SG, GE])
        feat = sb("feat", [P, 2, GE])
        hid = sb("hid", [HID, 2, GE])
        runmax = sb("runmax", [C, 2, GE])
        rows = [sb(f"rows{u}", [P, SG, TG * C]) for u in range(2)]
        assert NP <= 2 * (SE + 1)
        best = kb2[0:C, 0:NP]
        pair_ix = sb("pair_ix", [P, 2], i32)
        pair = sb("pair", [P, 2, C])
        dst_row = sb("dst_row", [1, P], i32)
        msg = sb("msg", [C, P])
        own_end = sb("own_end", [P, NB], i32)
        end_n = sb("end_n", [P, NB], i32)
        end_p = sb("end_p", [P, NB], i32)
        last_f = sb("last_f", [P, NB])
        last_ix = sb("last_ix", [P, NB], i32)
        valid = sb("valid", [P, NB])
        agg = sb("agg", [P, NB, C])
        mu = sb("mu", [P, NB])
        var = sb("var", [P, NB])

        ps_feat = pb("ps_feat", [P, 2, GE])
        ps_hid = pb("ps_hid", [HID, 2, GE])
        ps_msg = pb("ps_msg", [P, 2, GE])
        ps_rows = pb("ps_rows", [P, 2, GE])
        CUM = slice(TG * C, TG * C + 2)
        assert TG * C + 2 <= GE
        ps_src = [ps_feat[:, 0, 0:P], ps_feat[:, 1, 0:P], ps_hid[:, 0, 0:P], ps_hid[:, 1, 0:P]]
        ps_order = ps_msg[0:1, 0, 0:P]
        ps_sum = ps_msg[:, 1, 0:C]
        ps_var = ps_rows[:, 0, 0:2]
        ps_bias = ps_rows[:, 1, 0:1]

        consts_ready = sem("consts_ready")
        zero_ready = sem("zero_ready")
        src_pad_ready, pads_ready = sem("src_pad_ready"), sem("pads_ready")
        src_in, src_pad_in = sem("src_in"), sem("src_pad_in")
        dst_in, x_in, win_in, par_in = sem("dst_in"), sem("x_in"), sem("win_in"), sem("par_in")
        xpad_out, keys_out, ends_zeroed = sem("xpad_out"), sem("keys_out"), sem("ends_zeroed")
        src_f_ready, src_ps, src_ix_ready = sem("src_f_ready"), sem("src_ps"), sem("src_ix_ready")
        keys_ready = sem("keys_ready")
        g_dst_out, g_dst_in, g_ix, g_pair_in = sem("g_dst_out"), sem("g_dst_in"), sem("g_ix"), sem("g_pair_in")
        g_feat_ps, g_feat, g_hid_ps, g_hid = sem("g_feat_ps"), sem("g_feat"), sem("g_hid_ps"), sem("g_hid")
        g_msg_ps, g_msg, g_merged = sem("g_msg_ps"), sem("g_msg"), sem("g_merged")
        g_rows_ps, g_rows, g_own, g_out = sem("g_rows_ps"), sem("g_rows"), sem("g_own"), sem("g_out")
        order_ready, order_ps, flag_ready = sem("order_ready"), sem("order_ps"), sem("flag_ready")
        sum_ps, xc_ready, sq_ready, var_ps = sem("sum_ps"), sem("xc_ready"), sem("sq_ready"), sem("var_ps")
        std_in, std_ready = sem("std_in"), sem("std_ready")
        fold_ready, bias_ps, weights_ready = sem("fold_ready"), sem("bias_ps"), sem("weights_ready")
        wkey_ready = sem("wkey_ready")
        dve_step = sem("dve_step")
        ix_copied = sem("ix_copied")
        ix_read = sem("ix_read")
        rows_in = [sem(f"rows_in{k}") for k in range(IG)]
        key_in = [sem(f"key_in{u}") for u in range(2)]
        xwin_in = [sem(f"xwin_in{u}") for u in range(2)]
        onehot_ready, reset_ready = sem("onehot_ready"), sem("reset_ready")
        feat_ps, feat_sb = sem("feat_ps"), sem("feat_sb")
        hid_ps, hid_sb = sem("hid_ps"), sem("hid_sb")
        msg_ps, run_ready = sem("msg_ps"), sem("run_ready")
        rows_ps, rows_sb = sem("rows_ps"), sem("rows_sb")
        run_out = [sem(f"run_out{u}") for u in range(2)]
        cnt_ready, cum_ps, cum_ready, ends_out = sem("cnt_ready"), sem("cum_ps"), sem("cum_ready"), sem("ends_out")
        ends_in, last_ready, agg_in = sem("ends_in"), sem("last_ready"), [sem(f"agg_in{c}") for c in range(7)]
        NCH = 7
        CH = NB // NCH
        tail_c, tail_sq, tail_var, tail_std, tail_out, y_out = (sem("tail_c"), sem("tail_sq"), sem("tail_var"),
                                                       sem("tail_std"), sem("tail_out"), sem("y_out"))

        block = ctx.enter_context(nc.Block())

        def overlapped(ap, start, rows_, width, stride):
            return bass.AP(tensor=ap.tensor, offset=start, ap=[[stride, rows_], [1, width]])

        @block.sync
        def _(sp):
            nfull = FULL_T // P
            sp.dma_start(src_t[:, 0:nfull, :], src[0:nfull * P * P].rearrange("(b t i) -> t b i", t=P, i=P)).then_inc(src_in, 16)
            sp.wait_ge(src_pad_ready, 1)
            left = FULL_T - nfull * P
            sp.dma_start(src_t[0:left, nfull, :],
                         src[nfull * P * P:FULL_T * P].rearrange("(t i) -> t i", i=P)).then_inc(src_pad_in, 16)
            if REST:
                sp.dma_start(src_t[left:left + 1, nfull, 0:REST],
                             src[FULL_T * P:E].rearrange("(t i) -> t i", t=1)).then_inc(src_pad_in, 16)
            sp.wait_ge(pads_ready, 1)
            sp.dma_start(dst_r[0:WIDE, :], overlapped(dst, 0, WIDE, EC + 1, EC)).then_inc(dst_in, 16)
            sp.dma_start(dst_r[WIDE:P - 1, :], overlapped(dst, WIDE * EC, P - 1 - WIDE, EC + 1, EC)).then_inc(dst_in, 16)
            sp.dma_start(dst_r[P - 1:P, 0:ELAST], dst[(P - 1) * EC:E].rearrange("(p t) -> p t", p=1)).then_inc(dst_in, 16)
            sp.wait_ge(pads_ready, 3)
            sp.dma_start(xn[0:WIDE, :, :], x[0:WIDE * NB, :].rearrange("(p t) c -> p t c", t=NB)).then_inc(x_in, 16)
            sp.dma_start(xn[WIDE:P - 1, :, :],
                         x[WIDE * NB:(P - 1) * NB, :].rearrange("(p t) c -> p t c", t=NB)).then_inc(x_in, 16)
            sp.dma_start(xn[P - 1:P, 0:NLAST, :],
                         x[(P - 1) * NB:N, :].rearrange("(p t) c -> p t c", p=1)).then_inc(x_in, 16)
            sp.wait_ge(x_in, 48)
            sp.dma_start(x_pad[0:NP, :].rearrange("(p t) c -> p t c", t=NB), xn[:, :, :]).then_inc(xpad_out, 16)
            sp.wait_ge(zero_ready, 3)
            sp.dma_start(x_pad[NP:NP + P, :], zeros[:, :]).then_inc(xpad_out, 16)
            sp.dma_start(ends_dram[0:NP + P].rearrange("(p t) -> p t", p=P), zeros_i[:, 0:NB + 1]).then_inc(ends_zeroed, 16)
            sp.dma_start(ends_dram[NP + P:NP + P + 1].rearrange("(p t) -> p t", p=1), zeros_i[0:1, 0:1]).then_inc(ends_zeroed, 16)
            sp.dma_start(keys_dram[0:1].rearrange("(p t) -> p t", p=1), front_key[:, :]).then_inc(keys_out, 16)
            sp.wait_ge(keys_ready, 1)
            sp.dma_start(keys_dram[1:EP + 1].rearrange("(p t) -> p t", t=EC), keys[:, :]).then_inc(keys_out, 16)
            sp.wait_ge(keys_out, 32)
            sp.wait_ge(xpad_out, 32)
            sp.wait_ge(flag_ready, 1)
            windowed = sp.value_load(in_order[0:1, 0:1], min_val=0, max_val=1)
            with sp.If(windowed == 1):
              with sp.Fori(0, ITERS) as it:
                  for u in range(2):
                      sp.wait_ge(reset_ready, it * IG + SG * (u + 1))
                      sp.dma_start(kb[u], keys_dram[bass.ds((it * 2 + u) * SE, SE + 1)].rearrange("(a e) -> a e", a=1)
                                   .to_broadcast([P, SE + 1])).then_inc(key_in[u], 16)
                      sp.wait_ge(feat_ps, it * IG + SG * (u + 1))
                      first = sp.value_load(win0[0:1, bass.ds(it * 2 + u, 1)], min_val=0, max_val=N)
                      sp.dma_start(xwin[u][:, :], x_pad[bass.ds(first, P), :]).then_inc(xwin_in[u], 16)
              sp.wait_ge(ends_out, CREDIT_DMA + 32 * ITERS)
            with sp.Else():
                sp.dma_start(dst_dram.rearrange("(p t) -> p t", t=EC), dst_r[:, 0:EC]).then_inc(g_dst_out, 16)
                sp.wait_ge(g_rows, NB)
                sp.wait_ge(g_own, 1)
                sp.dma_start(run_dram[0:NP, :].rearrange("(p t) c -> p t c", t=NB), agg[:, :, :]).then_inc(g_out, 16)
                sp.dma_start(ends_dram[1:NP + 1].rearrange("(p t) -> p t", t=NB), own_end[:, :]).then_inc(g_out, 16)
                sp.wait_ge(g_out, 32)
            sp.dma_start(end_n[:, :], ends_dram[1:NP + 1].rearrange("(p t) -> p t", t=NB)).then_inc(ends_in, 16)
            sp.dma_start(end_p[:, :], ends_dram[0:NP].rearrange("(p t) -> p t", t=NB)).then_inc(ends_in, 16)
            for c in range(NCH):
                sp.wait_ge(tail_out, c + 1)
                t0, t1 = c * CH, (c + 1) * CH
                sp.dma_start(out[0:WIDE * NB, :].rearrange("(p t) c -> p t c", t=NB)[:, t0:t1, :],
                             agg[0:WIDE, t0:t1, :]).then_inc(y_out, 16)
                sp.dma_start(out[WIDE * NB:(P - 1) * NB, :].rearrange("(p t) c -> p t c", t=NB)[:, t0:t1, :],
                             agg[WIDE:P - 1, t0:t1, :]).then_inc(y_out, 16)
            sp.dma_start(out[(P - 1) * NB:N, :].rearrange("(p t) c -> p t c", p=1),
                         agg[P - 1:P, 0:NLAST, :]).then_inc(y_out, 16)
            sp.wait_ge(y_out, 16 * (2 * NCH + 1))

        @block.gpsimd
        def _(pool):
            pool.memset(src_t[:, FULL_T // P, :], 0).then_inc(src_pad_ready, 1)
            pool.memset(ident[:, :], 0.0).then_inc(consts_ready, 1)
            pool.memset(tri[:, :], 1.0).then_inc(consts_ready, 1)
            pool.wait_ge(consts_ready, 2)
            pool.affine_select(out=ident[:, :], in_=ident[:, :], compare_op=ALU.not_equal, fill=1.0, base=0,
                               pattern=[[-1, P]], channel_multiplier=1).then_inc(consts_ready, 1)
            pool.affine_select(out=tri[:, :], in_=tri[:, :], compare_op=ALU.is_ge, fill=0.0, base=0,
                               pattern=[[1, P]], channel_multiplier=-1).then_inc(consts_ready, 1)
            pool.iota(slot_col[:, :], pattern=[[0, 1]], base=0, channel_multiplier=1,
                      allow_small_or_imprecise_dtypes=True).then_inc(consts_ready, 1)
            pool.iota(sb_base[:, :], pattern=[[SE, NSB]], base=0, channel_multiplier=0,
                      allow_small_or_imprecise_dtypes=True).then_inc(consts_ready, 1)
            pool.wait_ge(src_ix_ready, TB)
            def gather(it):
                for u in range(2):
                    pool.wait_ge(feat_ps, it * IG + SG * (u + 1))
                    pool.tensor_copy(ix[u][:, :], src_ix[:, bass.ds((it * 2 + u) * SG * TG, SG * TG)]).then_inc(ix_copied, SG)
                    pool.wait_ge(src_ix_ready, TB)
                    pool.wait_ge(ix_copied, it * IG + SG * (u + 1))
                    for g in range(SG):
                        for t in range(TG):
                            col = g * TG + t
                            pool.indirect_dma_start(xs[:, u * SG + g, t, :], None, x[:, :],
                                                    bass.IndirectOffsetOnAxis(ap=ix[u][:, col:col + 1], axis=0))\
                                .then_inc(rows_in[u * SG + g], 16)

            gather(0)
            pool.wait_ge(flag_ready, 1)
            windowed = pool.value_load(in_order[0:1, 0:1], min_val=0, max_val=1)
            with pool.If(windowed == 1):
                with pool.Fori(1, ITERS) as it:
                    gather(it)
                for u in range(2):
                    pool.wait_ge(run_out[u], CREDIT_DMA + 16 * ITERS)
            with pool.Else():
                pool.iota(own_end[:, :], pattern=[[1, NB]], base=1, channel_multiplier=NB).then_inc(g_own, 1)
                with pool.Fori(0, GT) as i:
                    pool.wait_ge(g_dst_in, i * 32 + 32)
                    pool.wait_ge(g_merged, i * P + 1)
                    pool.tensor_copy(pair_ix[:, 0:1], src_ix[:, bass.ds(i, 1)]).then_inc(g_ix, 32)
                    pool.wait_ge(src_ix_ready, TB)
                    pool.wait_ge(g_ix, i * 32 + 32)
                    for side in range(2):
                        pool.indirect_dma_start(pair[:, side, :], None, x_pad[:, :],
                                                bass.IndirectOffsetOnAxis(ap=pair_ix[:, side:side + 1], axis=0)).then_inc(g_pair_in, 16)
                pool.wait_ge(g_out, 32)
            pool.wait_ge(last_ready, 1)
            for c in range(NCH):
                for t in range(c * CH, (c + 1) * CH):
                    pool.indirect_dma_start(agg[:, t, :], None, run_dram[:, :],
                                            bass.IndirectOffsetOnAxis(ap=last_ix[:, t:t + 1], axis=0)).then_inc(agg_in[c], 16)

        @block.scalar
        def _(act):
            act.wait_ge(pads_ready, 2)
            act.dma_start(win0[:, 1:NSB], bass.AP(tensor=dst.tensor, offset=SE, ap=[[0, P], [SE, NSB - 1], [1, 1]]),
                          allow_slow_non_contiguous=True).then_inc(win_in, 16)
            for h in range(2):
                act.dma_start(w_raw[h * C:(h + 1) * C, :], W1[C:2 * C, :]).then_inc(par_in, 16)
                act.dma_start(gam[h * C:(h + 1) * C, :], gamma.rearrange("(c a) -> c a", a=1)).then_inc(par_in, 16)
                act.dma_start(bet[h * C:(h + 1) * C, :], beta.rearrange("(c a) -> c a", a=1)).then_inc(par_in, 16)
            act.dma_start(w_a[C:2 * C, :], W1[0:C, :]).then_inc(par_in, 16)
            act.dma_start(w2[:, :], W2).then_inc(par_in, 16)
            act.dma_start(b1c[:, :], b1.rearrange("(c a) -> c a", a=1)).then_inc(par_in, 16)
            act.dma_start(b2b[:, :], b2.rearrange("(a c) -> a c", a=1).to_broadcast([P, C])).then_inc(par_in, 16)
            act.sem_inc(rows_sb, CREDIT_ST)
            act.sem_inc(ends_out, CREDIT_DMA)
            for u in range(2):
                act.sem_inc(run_out[u], CREDIT_DMA)
            act.wait_ge(xc_ready, 1)
            act.activation(xc[:, :, :], xc[:, :, :], ACT.Square).then_inc(sq_ready, 1)
            act.wait_ge(std_in, 1)
            act.activation(bn[:, 2:3], bn[:, 1:2], ACT.Sqrt).then_inc(std_ready, 1)
            act.wait_ge(weights_ready, 1)
            act.wait_ge(ends_zeroed, 32)
            act.wait_ge(flag_ready, 1)
            windowed = act.value_load(in_order[0:1, 0:1], min_val=0, max_val=1)
            with act.If(windowed == 1):
                with act.Fori(0, ITERS) as it:
                    base = it * IG
                    for k in range(IG + 4):
                        if k < IG:
                            act.wait_ge(feat_ps, base + (IG + k + 1))
                            if k >= 2:
                                act.wait_ge(hid_ps, base + (k - 1))
                            act.activation(feat[:, k % 2, :], ps_feat[:, k % 2, :], ACT.Copy).then_inc(feat_sb, 1)
                        j = k - 1
                        if 0 <= j < IG:
                            act.wait_ge(hid_ps, base + (j + 1))
                            if j >= 2:
                                act.wait_ge(msg_ps, base + (j - 1))
                            act.activation(hid[:, j % 2, :], ps_hid[:, j % 2, :], ACT.Relu,
                                           bias=bias1[:, :]).then_inc(hid_sb, 1)
                        j = k - 4
                        if 0 <= j < IG:
                            u, g = divmod(j, SG)
                            if g == 0:
                                act.wait_ge(run_out[u], it * 16 + CREDIT_DMA)
                            act.wait_ge(rows_ps, base + (j + 1))
                            act.activation(rows[u][:, g, :], ps_rows[:, j % 2, 0:TG * C], ACT.Copy).then_inc(rows_sb, 1)
                            if g == SG - 1:
                                act.wait_ge(rows_sb, base + (CREDIT_ST + j + 1))
                                act.dma_start(run_dram[bass.ds((it * 2 + u) * SE, SE), :]
                                              .rearrange("(g p t) c -> p g (t c)", p=P, t=TG), rows[u][:, :, :]).then_inc(run_out[u], 16)
                    act.wait_ge(cum_ready, it + (CREDIT_CUM + 1))
                    for u in range(2):
                        first = act.value_load(win0[0:1, bass.ds(it * 2 + u, 1)], min_val=0, max_val=N)
                        act.wait_ge(ends_out, it * 32 + (CREDIT_DMA + 16 * u))
                        act.dma_start(ends_dram[bass.ds(first + 1, P)].rearrange("(p a) -> p a", a=1),
                                      cum_i[:, u:u + 1]).then_inc(ends_out, 16)
            with act.Else():
                act.wait_ge(g_dst_out, 16)
                with act.Fori(0, GT) as i:
                    act.wait_ge(g_merged, i * P + 1)
                    act.dma_start(pair_ix[:, 1:2], dst_dram[bass.ds(i * P, P)].rearrange("(p a) -> p a", a=1)).then_inc(g_dst_in, 16)
                    act.dma_start(dst_row[:, :], dst_dram[bass.ds(i * P, P)].rearrange("(a e) -> a e", a=1)).then_inc(g_dst_in, 16)
                    act.wait_ge(g_feat_ps, i + 1)
                    act.activation(feat[:, 0, 0:P], ps_feat[:, 0, 0:P], ACT.Copy).then_inc(g_feat, 1)
                    act.wait_ge(g_hid_ps, i + 1)
                    act.activation(hid[:, 0, 0:P], ps_hid[:, 0, 0:P], ACT.Relu, bias=bias1[:, :]).then_inc(g_hid, 1)
                for t in range(NB):
                    act.wait_ge(g_rows_ps, t + 1)
                    act.activation(agg[:, t, :], ps_rows[:, t % 2, 0:C], ACT.Copy).then_inc(g_rows, 1)
            for c in range(NCH):
                sl = slice(c * CH, (c + 1) * CH)
                act.wait_ge(tail_c, c + 1)
                act.activation(xc[:, sl, :], xn[:, sl, :], ACT.Square).then_inc(tail_sq, 1)
                act.wait_ge(tail_var, c + 1)
                act.activation(mu[:, sl], var[:, sl], ACT.Sqrt).then_inc(tail_std, 1)

        @block.vector
        def _(dve):
            done = [0]

            def chain(ins):
                done[0] += 1
                ins.then_inc(dve_step, 1)
                dve.wait_ge(dve_step, done[0])

            dve.memset(dst_r[:, :], N).then_inc(pads_ready, 1)
            dve.memset(win0[:, :], N).then_inc(pads_ready, 1)
            dve.memset(xn[:, :, :], 0.0).then_inc(pads_ready, 1)
            dve.memset(zeros[:, :], 0.0).then_inc(zero_ready, 1)
            dve.memset(zeros_i[:, :], 0).then_inc(zero_ready, 1)
            dve.memset(front_key[:, :], -SCALE).then_inc(zero_ready, 1)
            dve.memset(runmax[:, 1, GE - 1:GE], SCALE)
            dve.memset(ones[:, :], 1.0).then_inc(zero_ready, 1)
            dve.sem_inc(reset_ready, IG)
            dve.sem_inc(cum_ready, CREDIT_CUM)
            dve.sem_inc(g_merged, 1)
            dve.wait_ge(src_in, 16)
            dve.wait_ge(src_pad_in, 32 if REST else 16)
            dve.tensor_copy(src_f[:, :, :], src_t[:, :, :]).then_inc(src_f_ready, 1)
            for b in range(TB):
                dve.wait_ge(src_ps, b + 1)
                dve.tensor_copy(src_ix[:, b * P:(b + 1) * P], ps_src[b % 4]).then_inc(src_ix_ready, 1)
            dve.wait_ge(dst_in, 48)
            dve.tensor_scalar(keys[:, :], dst_r[:, 0:EC], SCALE, None, ALU.mult).then_inc(keys_ready, 1)
            chain(dve.tensor_tensor(step[:, :], dst_r[:, 1:EC + 1], dst_r[:, 0:EC], ALU.subtract))
            dve.wait_ge(win_in, 16)
            chain(dve.memset(win0[:, 0:1], 0))
            chain(dve.tensor_tensor(win_step[:, :], win0[:, 1:NSB + 1], win0[:, 0:NSB], ALU.subtract))
            chain(dve.tensor_reduce(order_col[:, 0:1], step[:, :], AX.X, ALU.min))
            chain(dve.tensor_reduce(order_col[:, 1:2], win_step[:, :], AX.X, ALU.max))
            chain(dve.tensor_scalar(order_col[:, 2:3], order_col[:, 1:2], -1.0, float(P - 1), ALU.mult, ALU.add))
            dve.tensor_tensor(order_col[:, 3:4], order_col[:, 0:1], order_col[:, 2:3], ALU.min).then_inc(order_ready, 1)
            dve.wait_ge(consts_ready, 6)
            dve.tensor_scalar(win_key[:, :], win0[:, 0:NSB], slot_col[:, :], SCALE, ALU.add, ALU.mult).then_inc(wkey_ready, 1)
            dve.wait_ge(order_ps, 1)
            chain(dve.tensor_reduce(order_min[:, :], ps_order, AX.X, ALU.min))
            dve.tensor_scalar(in_order[:, :], order_min[:, :], 0.0, None, ALU.is_ge).then_inc(flag_ready, 1)
            dve.wait_ge(sum_ps, 1)
            chain(dve.tensor_scalar(mean_b[:, :], ps_sum, 1.0 / N, None, ALU.mult))
            dve.tensor_tensor(xc[:, :, :], xn[:, :, :], mean_b[:, :].rearrange("p (a c) -> p a c", a=1).to_broadcast([P, NB, C]),
                              ALU.subtract).then_inc(xc_ready, 1)
            dve.wait_ge(var_ps, 1)
            dve.tensor_scalar(bn[:, 1:2], ps_var[:, 0:1], 1.0 / N, EPS, ALU.mult, ALU.add).then_inc(std_in, 1)
            chain(dve.tensor_scalar(bn[:, 0:1], ps_var[:, 1:2], 1.0 / N, None, ALU.mult))
            dve.wait_ge(std_ready, 1)
            dve.wait_ge(par_in, 160)
            chain(dve.reciprocal(bn[:, 3:4], bn[:, 2:3]))
            chain(dve.tensor_tensor(bn[:, 4:5], bn[:, 3:4], gam[:, :], ALU.mult))
            chain(dve.tensor_tensor(bn[:, 3:4], bn[:, 0:1], bn[:, 4:5], ALU.mult))
            chain(dve.tensor_tensor(bn[:, 5:6], bet[:, :], bn[:, 3:4], ALU.subtract))
            chain(dve.tensor_tensor(w_raw[C:2 * C, :], w_a[C:2 * C, :], w_raw[C:2 * C, :], ALU.subtract))
            dve.tensor_scalar(w_cat[:, :], w_raw[:, :], bn[:, 4:5], None, ALU.mult).then_inc(fold_ready, 1)
            dve.wait_ge(bias_ps, 1)
            dve.tensor_tensor(bias1[:, :], ps_bias, b1c[:, :], ALU.add).then_inc(weights_ready, 1)
            dve.wait_ge(wkey_ready, 1)
            dve.wait_ge(flag_ready, 1)
            windowed = dve.value_load(in_order[0:1, 0:1], min_val=0, max_val=1)
            with dve.If(windowed == 1):
                with dve.Fori(0, ITERS) as it:
                    base = it * IG
                    for k in range(IG + 3):
                        if k < IG:
                            u, g = divmod(k, SG)
                            e0 = 1 + g * GE
                            if g == 0:
                                dve.wait_ge(key_in[u], it * 16 + 16)
                            if k >= 2:
                                dve.wait_ge(feat_ps, base + (IG + k - 1))
                            dve.tensor_scalar(onehot[:, k % 2, :], kb[u][:, e0:e0 + GE], win_key[:, bass.ds(it * 2 + u, 1)],
                                              0.0, ALU.is_equal, ALU.add, accum_out=cnt[:, u, g:g + 1]).then_inc(onehot_ready, 1)
                            dve.tensor_tensor(reset[:, g, :], kb[u][0:C, e0:e0 + GE], kb[u][0:C, e0 - 1:e0 - 1 + GE],
                                              ALU.subtract).then_inc(reset_ready, 1)
                        j = k - 3
                        if 0 <= j < IG:
                            dve.wait_ge(msg_ps, base + (j + 1))
                            dve.wait_ge(reset_ready, base + (IG + j + 1))
                            if j >= 2:
                                dve.wait_ge(rows_ps, base + (j - 1))
                            if j > 0:
                                dve.wait_ge(run_ready, base + j)
                            dve.tensor_tensor_scan(runmax[:, j % 2, :], reset[:, j % SG, :], ps_msg[0:C, j % 2, :],
                                                   runmax[:, (j + 1) % 2, GE - 1:GE], ALU.add, ALU.max).then_inc(run_ready, 1)
                    dve.wait_ge(onehot_ready, base + IG)
                    dve.tensor_reduce(cnt2[:, :], cnt[:, :, :], AX.X, ALU.add).then_inc(cnt_ready, 1)
                    dve.wait_ge(cum_ps, it + 1)
                    dve.wait_ge(ends_out, it * 32 + CREDIT_DMA)
                    dve.tensor_tensor(cum_i[:, :], ps_rows[:, 0, CUM], sb_base[:, bass.ds(it * 2, 2)], ALU.add).then_inc(cum_ready, 1)
            with dve.Else():
                dve.memset(best, SCALE).then_inc(g_msg, 1)
                with dve.Fori(0, GT) as i:
                    dve.wait_ge(g_dst_in, i * 32 + 32)
                    dve.wait_ge(g_msg_ps, i + 1)
                    dve.tensor_copy(msg[:, :], ps_msg[0:C, 0, 0:P]).then_inc(g_msg, 1)
                    with dve.Fori(0, P) as e:
                        node = dve.value_load(dst_row[0:1, bass.ds(e, 1)], min_val=0, max_val=N)
                        dve.wait_ge(g_msg, i + 2)
                        dve.wait_ge(g_merged, i * P + e + 1)
                        dve.tensor_tensor(best[:, bass.ds(node, 1)], best[:, bass.ds(node, 1)], msg[:, bass.ds(e, 1)],
                                          ALU.max).then_inc(g_merged, 1)
            dve.wait_ge(ends_in, 32)
            dve.tensor_tensor(valid[:, :], end_n[:, :], end_p[:, :], ALU.is_gt)
            chain(dve.tensor_scalar(last_f[:, :], end_n[:, :], -1.0, 0.0, ALU.add, ALU.max))
            dve.tensor_copy(last_ix[:, :], last_f[:, :]).then_inc(last_ready, 1)
            for c in range(NCH):
                sl = slice(c * CH, (c + 1) * CH)

                def over(ap):
                    return ap.rearrange("p (t a) -> p t a", a=1).to_broadcast([P, CH, C])

                dve.wait_ge(agg_in[c], 16 * CH)
                chain(dve.tensor_tensor(agg[:, sl, :], agg[:, sl, :],
                                        b2b[:, :].rearrange("p (a c) -> p a c", a=1).to_broadcast([P, CH, C]), ALU.add))
                chain(dve.scalar_tensor_tensor(agg[:, sl, :], agg[:, sl, :], 0.0, over(valid[:, sl]), ALU.max, ALU.mult))
                chain(dve.tensor_tensor(agg[:, sl, :], agg[:, sl, :], xn[:, sl, :], ALU.add))
                chain(dve.tensor_reduce(mu[:, sl], agg[:, sl, :], AX.X, ALU.add))
                chain(dve.tensor_scalar(mu[:, sl], mu[:, sl], 1.0 / C, None, ALU.mult))
                dve.tensor_tensor(xn[:, sl, :], agg[:, sl, :], over(mu[:, sl]), ALU.subtract).then_inc(tail_c, 1)
                dve.wait_ge(tail_sq, c + 1)
                chain(dve.tensor_reduce(var[:, sl], xc[:, sl, :], AX.X, ALU.add))
                dve.tensor_scalar(var[:, sl], var[:, sl], 1.0 / C, EPS, ALU.mult, ALU.add).then_inc(tail_var, 1)
                dve.wait_ge(tail_std, c + 1)
                chain(dve.reciprocal(var[:, sl], mu[:, sl]))
                dve.tensor_tensor(agg[:, sl, :], xn[:, sl, :], over(var[:, sl]), ALU.mult).then_inc(tail_out, 1)

        @block.tensor
        def _(pe):
            pe.sem_inc(feat_ps, IG)
            pe.wait_ge(consts_ready, 6)
            pe.wait_ge(src_f_ready, 1)
            for b in range(TB):
                if b >= 4:
                    pe.wait_ge(src_ix_ready, b - 3)
                pe.transpose(ps_src[b % 4], src_f[:, b, :], ident[:, :]).then_inc(src_ps, 1)
            pe.wait_ge(src_ix_ready, TB)
            pe.wait_ge(order_ready, 1)
            pe.transpose(ps_order, order_col[:, 3:4], ident[:, :]).then_inc(order_ps, 1)
            pe.wait_ge(x_in, 48)
            pe.wait_ge(zero_ready, 4)
            for t in range(NB):
                q = P if t < NLAST else P - 1
                last = pe.matmul(ps_sum, ones[0:q, :], xn[0:q, t, :], start=(t == 0), stop=(t == NB - 1))
            last.then_inc(sum_ps, 1)
            pe.wait_ge(flag_ready, 1)
            pe.wait_ge(sq_ready, 1)
            for col, of in ((0, xc), (1, xn)):
                for h in range(2):
                    for t in range(NB):
                        q = P if t < NLAST else P - 1
                        last = pe.matmul(ps_var[h * C:(h + 1) * C, col:col + 1], of[0:q, t, :], ones[0:q, 0:1],
                                         start=(t == 0), stop=(t == NB - 1))
            last.then_inc(var_ps, 1)
            pe.wait_ge(fold_ready, 1)
            pe.matmul(ps_bias, w_raw[:, :], bn[:, 5:6], start=True, stop=True).then_inc(bias_ps, 1)
            pe.wait_ge(weights_ready, 1)
            pe.wait_ge(flag_ready, 1)
            windowed = pe.value_load(in_order[0:1, 0:1], min_val=0, max_val=1)
            with pe.If(windowed == 1):
                with pe.Fori(0, ITERS) as it:
                    base = it * IG
                    for k in range(IG + 4):
                        if k < IG:
                            u, g = divmod(k, SG)
                            if k >= 2:
                                pe.wait_ge(feat_sb, base + (k - 1))
                            pe.wait_ge(rows_in[k], it * (16 * TG) + 16 * TG)
                            if g == 0:
                                pe.wait_ge(xwin_in[u], it * 16 + 16)
                            pe.wait_ge(onehot_ready, base + (k + 1))
                            pe.matmul(ps_feat[C:2 * C, k % 2, :], xwin[u][:, :], onehot[:, k % 2, :], start=True, stop=True)
                            for t in range(TG):
                                last = pe.transpose(ps_feat[0:C, k % 2, t * P:(t + 1) * P], xs[:, k, t, :], ident[:, :])
                            last.then_inc(feat_ps, 1)
                        j = k - 1
                        if 0 <= j < IG:
                            pe.wait_ge(feat_sb, base + (j + 1))
                            if j >= 2:
                                pe.wait_ge(hid_sb, base + (j - 1))
                            pe.matmul(ps_hid[:, j % 2, :], w_cat[:, :], feat[:, j % 2, :], start=True, stop=True).then_inc(hid_ps, 1)
                        j = k - 2
                        if 0 <= j < IG:
                            pe.wait_ge(hid_sb, base + (j + 1))
                            if j >= 2:
                                pe.wait_ge(run_ready, base + (j - 1))
                            if j == 2:
                                pe.wait_ge(cum_ready, it + CREDIT_CUM)
                            pe.matmul(ps_msg[0:C, j % 2, :], w2[:, :], hid[:, j % 2, :], start=True, stop=True).then_inc(msg_ps, 1)
                        j = k - 4
                        if 0 <= j < IG:
                            pe.wait_ge(consts_ready, 6)
                            pe.wait_ge(run_ready, base + (j + 1))
                            pe.wait_ge(rows_sb, base + (j + 1))
                            strided = runmax[:, j % 2, :].rearrange("c (p t) -> c t p", t=TG)
                            for t in range(TG):
                                last = pe.transpose(ps_rows[:, j % 2, t * C:(t + 1) * C], strided[:, t, :], ident[0:C, 0:C])
                            last.then_inc(rows_ps, 1)
                    pe.wait_ge(cnt_ready, it + 1)
                    pe.wait_ge(rows_sb, base + (CREDIT_ST + IG - 1))
                    pe.matmul(ps_rows[:, 0, CUM], tri[:, :], cnt2[:, :], start=True, stop=True).then_inc(cum_ps, 1)
            with pe.Else():
                with pe.Fori(0, GT) as i:
                    pe.wait_ge(g_pair_in, i * 32 + 32)
                    pe.transpose(ps_feat[:, 0, 0:P], pair[:, :, :].rearrange("p s c -> p (s c)"), ident[:, :]).then_inc(g_feat_ps, 1)
                    pe.wait_ge(g_feat, i + 1)
                    pe.matmul(ps_hid[:, 0, 0:P], w_cat[:, :], feat[:, 0, 0:P], start=True, stop=True).then_inc(g_hid_ps, 1)
                    pe.wait_ge(g_hid, i + 1)
                    pe.matmul(ps_msg[0:C, 0, 0:P], w2[:, :], hid[:, 0, 0:P], start=True, stop=True).then_inc(g_msg_ps, 1)
                pe.wait_ge(g_merged, GT * P + 1)
                by_col = best.rearrange("c (p t) -> c t p", t=NB)
                for t in range(NB):
                    if t >= 2:
                        pe.wait_ge(g_rows, t - 1)
                    pe.transpose(ps_rows[:, t % 2, 0:C], by_col[:, t, :], ident[0:C, 0:C]).then_inc(g_rows_ps, 1)



_INS = ["x", "src", "dst", "L0_gnn_gamma", "L0_gnn_beta", "L0_gnn_W1", "L0_gnn_b1", "L0_gnn_W2", "L0_gnn_b2"]


def kernel(**inputs):
    import concourse.bacc as bacc
    from concourse.bass_utils import run_bass_kernel_spmd as run

    nc = bacc.Bacc("TRN2", target_bir_lowering=False, num_devices=1)
    arrays, args = {}, []
    for name in _INS:
        a = np.ascontiguousarray(inputs[name])
        arrays[f"in_{name}"] = a
        args.append(nc.dram_tensor(f"in_{name}", a.shape, mybir.dt.from_np(a.dtype), kind="ExternalInput").ap())
    out = nc.dram_tensor("out_0", inputs["x"].shape, mybir.dt.float32, kind="ExternalOutput").ap()
    edge_conv_program(nc, *args, out)
    r = run(nc, [arrays], core_ids=[0])
    return r.results[0]["out_0"]
```

```python
import concourse.bass as bass
import concourse.mybir as mybir
import numpy as np
from contextlib import ExitStack


def edge_conv_program(nc, x, src, dst, gamma, beta, W1, b1, W2, b2, out):
    f32, i32, bf16 = mybir.dt.float32, mybir.dt.int32, mybir.dt.bfloat16
    ALU, ACT, AX = mybir.AluOpType, mybir.ActivationFunctionType, mybir.AxisListType

    P = 128
    N, C = x.shape
    E = src.shape[0]
    HID = W1.shape[1]
    TG = 4
    GE = TG * P
    SG = 7
    ST = SG * TG
    SE = SG * GE
    NSB = -(-E // (2 * SE)) * 2
    ITERS, IG = NSB // 2, 2 * SG
    EP = NSB * SE
    TILES = EP // P
    GT = -(-E // P)
    TB = -(-TILES // P)
    FULL_T = E // P
    REST = E - FULL_T * P
    PN = max(p for p in range(1, P + 1) if N % p == 0)
    TN = N // PN
    C1 = C + 1
    ELAST = E - (NSB - 1) * SE
    SMID = (NSB - 2) // 16 * 16
    SCALE = -(2.0 ** 112)
    EPS = 1e-5
    CREDIT_DMA = 16
    AT_ACC, AT_CENTRE, AT_STD, AT_NORM = [SG + 4, IG + 4], [SG + 5, IG + 4], [SG + 6, IG + 5], [SG + 7, IG + 5]
    ND = 6
    KT = GE // NSB
    assert N >= P and 0 < ELAST <= SE and TB * P >= TILES and FULL_T >= P >= 2 * ST and -(-ST // KT) <= 4

    keys_dram = nc.dram_tensor("keys_dram", [NSB, SE + 1], bf16, kind="Internal").ap()
    dst_dram = nc.dram_tensor("dst_dram", [EP], i32, kind="Internal").ap()

    ctx = ExitStack()
    with ctx:
        def sb(name, shape, dt=f32):
            return ctx.enter_context(nc.sbuf_tensor(name, shape, dt))

        def pb(name, shape, dt=f32):
            return ctx.enter_context(nc.psum_tensor(name, shape, dt))

        def sem(name):
            return ctx.enter_context(nc.semaphore(name))

        ident = sb("ident", [P, P])
        ones = sb("ones", [P, P])
        eps_col = sb("eps_col", [P, 1])
        slot_col = sb("slot_col", [P, 1])
        slot_row = sb("slot_row", [P, P])
        src_t = sb("src_t", [P, TB, P], i32)
        src_f = sb("src_f", [P, TB, P])
        src_ix = sb("src_ix", [P, TB * P], i32)
        dst_r = sb("dst_r", [NSB, SE + 2], i32)
        win_col = sb("win_col", [NSB, 1])
        keys = sb("keys", [NSB, SE + 1], bf16)
        step = sb("step", [NSB, SE + 1], bf16)
        last_r = sb("last_r", [NSB, SE])
        last_key = sb("last_key", [P, ST, NSB])
        first_dst = sb("first_dst", [1, NSB + 1], i32)
        win0 = sb("win0", [1, NSB + 1], i32)
        win_step = sb("win_step", [1, NSB])
        moved = sb("moved", [1, NSB])
        carry_col = sb("carry_col", [P, NSB])
        slot_key = sb("slot_key", [P, 1])
        slot_keys = sb("slot_keys", [P, P])
        order_col = sb("order_col", [NSB, 1])
        order = sb("order", [1, 4])
        in_order = sb("in_order", [1, 1], i32)
        xn = sb("xn", [P, TN, C])
        xc = sb("xc", [P, TN, C])
        part = sb("part", [P, C])
        part_sq = sb("part_sq", [P, C])
        mean_b = sb("mean_b", [P, C])
        w_raw = sb("w_raw", [P, HID])
        w_a = sb("w_a", [P, HID])
        w_cat = sb("w_cat", [P, HID])
        w2 = sb("w2", [HID, C])
        b1c = sb("b1c", [HID, 1])
        bias1 = sb("bias1", [HID, 1])
        b2b = sb("b2b", [P, C])
        gam = sb("gam", [P, 1])
        bet = sb("bet", [P, 1])
        bn = sb("bn", [P, 6])
        ix = [sb(f"ix{u}", [P, ST], i32) for u in range(2)]
        xs = sb("xs", [P, IG, TG, C])
        KB0 = 16
        kb = [sb(f"kb{u}", [P, KB0 + SE], bf16) for u in range(2)]
        xwin = [sb(f"xwin{u}", [P, C]) for u in range(2)]
        xw = [sb(f"xw{u}", [P, 3, C], bf16) for u in range(2)]
        xw_rest = sb("xw_rest", [P, C])
        onehot = sb("onehot", [P, 2, GE], bf16)
        reset = sb("reset", [C, SG, GE], bf16)
        feat = sb("feat", [P, 2, GE])
        hid = sb("hid", [HID, 2, GE])
        runmax = sb("runmax", [C, 2, GE])
        rows = sb("rows", [P, 2, TG, C1])
        pick = sb("pick", [P, 2, TG, P])
        shift = sb("shift", [P, P])
        acc = sb("acc", [P, C1])
        res = sb("res", [P, C])
        cen = sb("cen", [P, C])
        cen_sq = sb("cen_sq", [P, C])
        norm = sb("norm", [P, 5])
        y = sb("y", [P, C])
        best = sb("best", [C1, N + 1])
        pair_dst = sb("pair_dst", [P, 1], i32)
        pair_ix = sb("pair_ix", [P, 2], i32)
        pair = sb("pair", [P, 2, C])
        dst_row = sb("dst_row", [1, P], i32)
        msg = sb("msg", [C1, P])

        ps_feat = pb("ps_feat", [P, 2, GE])
        ps_hid = pb("ps_hid", [HID, 2, GE])
        ps_msg = pb("ps_msg", [P, 2, GE])
        ps_rows = pb("ps_rows", [P, GE])
        ps_acc = pb("ps_acc", [P, GE])
        ps_src = [ps_feat[:, 0, 0:P], ps_feat[:, 1, 0:P], ps_hid[:, 0, 0:P], ps_hid[:, 1, 0:P]]
        ps_last = [ps_feat[:, 0, :], ps_feat[:, 1, :], ps_hid[:, 0, :], ps_hid[:, 1, :]]
        ps_order = ps_msg[0:1, 0, 0:NSB]
        ps_sum = ps_msg[:, 1, 0:C]
        ps_var = ps_rows[:, 0:2]
        ps_moved = ps_acc[:, 0:NSB]
        ps_bias = ps_acc[:, 0:1]
        LAST_CUTS = [(b, b * KT, min(ST, (b + 1) * KT)) for b in range(-(-ST // KT))]

        consts_ready = sem("consts_ready")
        ones_ready = sem("ones_ready")
        src_pad_ready, pads_ready = sem("src_pad_ready"), sem("pads_ready")
        src_first, src_in, src_pad_in = sem("src_first"), sem("src_in"), sem("src_pad_in")
        dst_in, x_in, win_in, par_in = sem("dst_in"), sem("x_in"), sem("win_in"), sem("par_in")
        keys_out = sem("keys_out")
        src_f_ready, src_ps, src_ix_ready = sem("src_f_ready"), sem("src_ps"), sem("src_ix_ready")
        keys_ready = sem("keys_ready")
        last_r_ready, last_ps, last_ready = sem("last_r_ready"), sem("last_ps"), sem("last_ready")
        g_dst_out, g_dst_in, g_ix, g_pair_in = sem("g_dst_out"), sem("g_dst_in"), sem("g_ix"), sem("g_pair_in")
        g_feat_ps, g_feat, g_hid_ps, g_hid = sem("g_feat_ps"), sem("g_feat"), sem("g_hid_ps"), sem("g_hid")
        g_msg_ps, g_msg, g_merged = sem("g_msg_ps"), sem("g_msg"), sem("g_merged")
        g_block = sem("g_block")
        order_ready, order_ps, flag_ready = sem("order_ready"), sem("order_ps"), sem("flag_ready")
        part_ready, sum_ps, xc_ready, sq_ready, var_ps = sem("part_ready"), sem("sum_ps"), sem("xc_ready"), sem("sq_ready"), sem("var_ps")
        std_in, std_ready = sem("std_in"), sem("std_ready")
        fold_ready, bias_ps, weights_ready = sem("fold_ready"), sem("bias_ps"), sem("weights_ready")
        slot_keys_ready = sem("slot_keys_ready")
        dve_step = sem("dve_step")
        ix_copied = sem("ix_copied")
        rows_in = [sem(f"rows_in{k}") for k in range(IG)]
        key_in = [sem(f"key_in{u}") for u in range(2)]
        xwin_in = [sem(f"xwin_in{u}") for u in range(2)]
        split_step = sem("split_step")
        onehot_ready, reset_ready = sem("onehot_ready"), sem("reset_ready")
        feat_ps, feat_sb = sem("feat_ps"), sem("feat_sb")
        hid_ps, hid_sb = sem("hid_ps"), sem("hid_sb")
        msg_ps, run_ready = sem("msg_ps"), sem("run_ready")
        rows_ps, rows_sb, pick_ready = sem("rows_ps"), sem("rows_sb"), sem("pick_ready")
        moved_ready, moved_ps, carry_ready, shift_ready = sem("moved_ready"), sem("moved_ps"), sem("carry_ready"), sem("shift_ready")
        acc_ps, acc_sb = sem("acc_ps"), sem("acc_sb")
        end_step, end_sq, end_std, y_ready, y_out = sem("end_step"), sem("end_sq"), sem("end_std"), sem("y_ready"), sem("y_out")

        block = ctx.enter_context(nc.Block())

        def overlapped(ap, start, rows_, width, stride):
            return bass.AP(tensor=ap.tensor, offset=start, ap=[[stride, rows_], [1, width]])

        def node_blocks(eng, body):
            with eng.Fori(0, N // P) as b:
                body(b, b * P)
            if N % P:
                body(N // P, N - P)

        @block.sync
        def _(sp):
            nfull = FULL_T // P
            sp.dma_start(src_t[:, 0, :], src[0:P * P].rearrange("(t i) -> t i", i=P)).then_inc(src_first, 16)
            if nfull > 1:
                sp.dma_start(src_t[:, 1:nfull, :],
                             src[P * P:nfull * P * P].rearrange("(b t i) -> t b i", t=P, i=P)).then_inc(src_in, 16)
            sp.wait_ge(src_pad_ready, 1)
            left = FULL_T - nfull * P
            sp.dma_start(src_t[0:left, nfull, :],
                         src[nfull * P * P:FULL_T * P].rearrange("(t i) -> t i", i=P)).then_inc(src_pad_in, 16)
            if REST:
                sp.dma_start(src_t[left:left + 1, nfull, 0:REST],
                             src[FULL_T * P:E].rearrange("(t i) -> t i", t=1)).then_inc(src_pad_in, 16)
            sp.wait_ge(pads_ready, 2)
            sp.dma_start(dst_r[0:1, 1:SE + 2], overlapped(dst, 0, 1, SE + 1, SE)).then_inc(dst_in, 16)
            if SMID:
                sp.dma_start(dst_r[1:1 + SMID, :], overlapped(dst, SE - 1, SMID, SE + 2, SE)).then_inc(dst_in, 16)
            sp.dma_start(dst_r[1 + SMID:NSB - 1, :],
                         overlapped(dst, (1 + SMID) * SE - 1, NSB - 2 - SMID, SE + 2, SE)).then_inc(dst_in, 16)
            sp.dma_start(dst_r[NSB - 1:NSB, 0:ELAST + 1], overlapped(dst, E - ELAST - 1, 1, ELAST + 1, SE)).then_inc(dst_in, 16)
            sp.dma_start(xn[0:PN, :, :], x.rearrange("(p t) c -> p t c", t=TN)).then_inc(x_in, 16)
            sp.wait_ge(keys_ready, 1)
            sp.dma_start(keys_dram, keys[:, :]).then_inc(keys_out, 16)
            sp.wait_ge(keys_out, 16)
            sp.wait_ge(flag_ready, 1)
            windowed = sp.value_load(in_order[0:1, 0:1], min_val=0, max_val=1)

            def load_keys(s, u):
                sp.dma_start(kb[u][:, KB0 - 1:KB0 + SE],
                             keys_dram[bass.ds(s, 1), :].to_broadcast([P, SE + 1])).then_inc(key_in[u], 16)

            def load_window(s, u):
                first = sp.value_load(win0[0:1, bass.ds(s, 1)], min_val=0, max_val=N - P)
                sp.dma_start(xwin[u][:, :], x[bass.ds(first, P), :]).then_inc(xwin_in[u], 16)

            def store_window(s):
                first = sp.value_load(win0[0:1, bass.ds(s, 1)], min_val=0, max_val=N - P)
                sp.wait_ge(y_ready, s + 1)
                sp.dma_start(out[bass.ds(first, P), :], y[:, :]).then_inc(y_out, 16)

            with sp.If(windowed == 1):
                for u in range(2):
                    load_keys(u, u)
                    load_window(u, u)
                with sp.Fori(0, ITERS - 1) as it:
                    for u in range(2):
                        sp.wait_ge(reset_ready, it * IG + SG * (u + 1))
                        load_keys(it * 2 + (2 + u), u)
                        sp.wait_ge(end_step, it * (2 * ND) + (ND * (u + 1) + 2))
                        load_window(it * 2 + (2 + u), u)
                        store_window(it * 2 + u)
                for u in range(2):
                    store_window(NSB - 2 + u)
                sp.wait_ge(y_out, CREDIT_DMA + 16 * NSB)
            with sp.Else():
                sp.dma_start(dst_dram.rearrange("(s e) -> s e", e=SE), dst_r[:, 1:SE + 1]).then_inc(g_dst_out, 16)

                def node_block(b, first):
                    sp.wait_ge(end_step, b * ND + 2)
                    sp.dma_start(xwin[0][:, :], x[bass.ds(first, P), :]).then_inc(xwin_in[0], 16)
                    sp.wait_ge(y_ready, b + 1)
                    sp.dma_start(out[bass.ds(first, P), :], y[:, :]).then_inc(y_out, 16)

                node_blocks(sp, node_block)
                sp.wait_ge(y_out, CREDIT_DMA + 16 * -(-N // P))

        @block.gpsimd
        def _(pool):
            pool.memset(src_t[:, FULL_T // P, :], 0).then_inc(src_pad_ready, 1)
            pool.memset(ident[:, :], 0.0).then_inc(consts_ready, 1)
            pool.wait_ge(consts_ready, 1)
            pool.affine_select(out=ident[:, :], in_=ident[:, :], compare_op=ALU.not_equal, fill=1.0, base=0,
                               pattern=[[-1, P]], channel_multiplier=1).then_inc(consts_ready, 1)
            pool.iota(slot_col[:, :], pattern=[[0, 1]], base=1, channel_multiplier=1,
                      allow_small_or_imprecise_dtypes=True).then_inc(consts_ready, 1)
            pool.iota(slot_row[:, :], pattern=[[1, P]], base=1, channel_multiplier=0,
                      allow_small_or_imprecise_dtypes=True).then_inc(consts_ready, 1)

            def gather(it):
                for u in range(2):
                    groups = it * IG + SG * (u + 1)
                    if not isinstance(groups, int):
                        groups = pool.to_reg(groups)
                    pool.wait_ge(ix_copied, 2 * SG)
                    pool.wait_ge(feat_ps, groups)
                    pool.wait_ge(ix_copied, groups)
                    for g in range(SG):
                        for t in range(TG):
                            col = g * TG + t
                            pool.indirect_dma_start(xs[:, u * SG + g, t, :], None, x[:, :],
                                                    bass.IndirectOffsetOnAxis(ap=ix[u][:, col:col + 1], axis=0))\
                                .then_inc(rows_in[u * SG + g], 16)

            gather(0)
            pool.wait_ge(flag_ready, 1)
            windowed = pool.value_load(in_order[0:1, 0:1], min_val=0, max_val=1)
            with pool.If(windowed == 1):
                with pool.Fori(1, ITERS) as it:
                    gather(it)
            with pool.Else():
                with pool.Fori(0, GT) as i:
                    pool.wait_ge(g_dst_in, i * 32 + 32)
                    pool.wait_ge(g_merged, i * P + 1)
                    pool.tensor_copy(pair_ix[:, 0:1], src_ix[:, bass.ds(i, 1)]).then_inc(g_ix, 16)
                    pool.tensor_scalar(pair_ix[:, 1:2], pair_dst[:, :], 0.0, float(N - 1), ALU.add, ALU.min).then_inc(g_ix, 16)
                    pool.wait_ge(src_ix_ready, TB)
                    pool.wait_ge(g_ix, i * 32 + 32)
                    for side in range(2):
                        pool.indirect_dma_start(pair[:, side, :], None, x[:, :],
                                                bass.IndirectOffsetOnAxis(ap=pair_ix[:, side:side + 1], axis=0)).then_inc(g_pair_in, 16)

        @block.scalar
        def _(act):
            def copy_ix(it, u):
                act.activation(ix[u][:, :], src_ix[:, bass.ds((it * 2 + u) * ST, ST)], ACT.Copy).then_inc(ix_copied, SG)

            def take_acc(s):
                act.wait_ge(acc_ps, s * SG + SG)
                act.wait_ge(end_step, s * ND + 1)
                act.activation(acc[:, :], ps_acc[:, 0:C1], ACT.Copy).then_inc(acc_sb, 1)

            def deviation(s):
                act.wait_ge(end_step, s * ND + (ND + 5))
                act.activation(cen_sq[:, :], cen[:, :], ACT.Square, accum_out=norm[:, 2:3]).then_inc(end_sq, 1)
                act.wait_ge(end_sq, s + 1)
                act.activation(norm[:, 3:4], norm[:, 2:3], ACT.Sqrt, bias=eps_col[:, :], scale=1.0 / C).then_inc(end_std, 1)

            act.wait_ge(pads_ready, 3)
            act.dma_start(first_dst[:, 1:NSB], bass.AP(tensor=dst.tensor, offset=SE, ap=[[0, 1], [SE, NSB - 1], [1, 1]]),
                          allow_slow_non_contiguous=True).then_inc(win_in, 16)
            for h in range(2):
                act.dma_start(w_raw[h * C:(h + 1) * C, :], W1[C:2 * C, :]).then_inc(par_in, 16)
                act.dma_start(gam[h * C:(h + 1) * C, :], gamma.rearrange("(c a) -> c a", a=1)).then_inc(par_in, 16)
                act.dma_start(bet[h * C:(h + 1) * C, :], beta.rearrange("(c a) -> c a", a=1)).then_inc(par_in, 16)
            act.dma_start(w_a[C:2 * C, :], W1[0:C, :]).then_inc(par_in, 16)
            act.dma_start(w2[:, :], W2).then_inc(par_in, 16)
            act.dma_start(b1c[:, :], b1.rearrange("(c a) -> c a", a=1)).then_inc(par_in, 16)
            act.dma_start(b2b[:, :], b2.rearrange("(a c) -> a c", a=1).to_broadcast([P, C])).then_inc(par_in, 16)
            act.sem_inc(acc_sb, 1)
            act.sem_inc(end_step, ND)
            act.sem_inc(y_out, CREDIT_DMA)
            act.wait_ge(xc_ready, 1)
            act.activation(xc[0:PN, :, :], xc[0:PN, :, :], ACT.Square).then_inc(sq_ready, 1)
            for b, t0, t1 in LAST_CUTS:
                act.wait_ge(last_ps, b + 1)
                act.activation(last_key[:, t0:t1, :], ps_last[b][:, 0:(t1 - t0) * NSB].rearrange("p (t s) -> p t s", s=NSB),
                               ACT.Copy).then_inc(last_ready, 1)
            act.wait_ge(std_in, 1)
            act.activation(bn[:, 2:3], bn[:, 1:2], ACT.Sqrt).then_inc(std_ready, 1)
            act.wait_ge(weights_ready, 1)
            act.wait_ge(src_ix_ready, TB)
            act.wait_ge(ones_ready, 4)
            act.wait_ge(flag_ready, 1)
            windowed = act.value_load(in_order[0:1, 0:1], min_val=0, max_val=1)
            with act.If(windowed == 1):
                with act.Fori(0, ITERS) as it:
                    base = it * IG
                    for k in range(IG + 6):
                        if k < IG:
                            act.wait_ge(feat_ps, base + (IG + k + 1))
                            if k >= 2:
                                act.wait_ge(hid_ps, base + (k - 1))
                            act.activation(feat[:, k % 2, :], ps_feat[:, k % 2, :], ACT.Copy).then_inc(feat_sb, 1)
                            if k % SG == SG - 1:
                                copy_ix(it + 1, k // SG)
                        j = k - 1
                        if 0 <= j < IG:
                            act.wait_ge(hid_ps, base + (j + 1))
                            if j >= 2:
                                act.wait_ge(msg_ps, base + (j - 1))
                            act.activation(hid[:, j % 2, :], ps_hid[:, j % 2, :], ACT.Relu,
                                           bias=bias1[:, :]).then_inc(hid_sb, 1)
                        j = k - 4
                        if 0 <= j < IG:
                            act.wait_ge(rows_ps, base + (j + 1))
                            if j >= 2:
                                act.wait_ge(acc_ps, base + (j - 1))
                            act.activation(rows[:, j % 2, :, 0:C], ps_rows[:, 0:TG * C].rearrange("p (t c) -> p t c", c=C),
                                           ACT.Copy).then_inc(rows_sb, 1)
                        if k in AT_ACC:
                            take_acc(it * 2 + AT_ACC.index(k))
                        if k in AT_STD:
                            deviation(it * 2 + AT_STD.index(k))
            with act.Else():
                act.wait_ge(g_dst_out, 16)
                with act.Fori(0, GT) as i:
                    act.wait_ge(g_merged, i * P + 1)
                    act.dma_start(pair_dst[:, :], dst_dram[bass.ds(i * P, P)].rearrange("(p a) -> p a", a=1)).then_inc(g_dst_in, 16)
                    act.dma_start(dst_row[:, :], dst_dram[bass.ds(i * P, P)].rearrange("(a e) -> a e", a=1)).then_inc(g_dst_in, 16)
                    act.wait_ge(g_feat_ps, i + 1)
                    act.activation(feat[:, 0, 0:P], ps_feat[:, 0, 0:P], ACT.Copy).then_inc(g_feat, 1)
                    act.wait_ge(g_hid_ps, i + 1)
                    act.activation(hid[:, 0, 0:P], ps_hid[:, 0, 0:P], ACT.Relu, bias=bias1[:, :]).then_inc(g_hid, 1)

                def node_block(b, first):
                    take_acc(b)
                    deviation(b)

                node_blocks(act, node_block)

        @block.vector
        def _(dve):
            done = [0]

            def chain(ins):
                done[0] += 1
                ins.then_inc(dve_step, 1)
                dve.wait_ge(dve_step, done[0])

            def centre(s, u, loads):
                n0 = s * ND + ND
                dve.wait_ge(acc_sb, s + 2)
                dve.scalar_tensor_tensor(res[:, :], b2b[:, :], acc[:, C:C1], acc[:, 0:C], ALU.mult, ALU.add).then_inc(end_step, 1)
                dve.wait_ge(xwin_in[u], loads * 16)
                dve.wait_ge(end_step, n0 + 1)
                dve.scalar_tensor_tensor(res[:, :], res[:, :], 0.0, xwin[u][:, :], ALU.max, ALU.add).then_inc(end_step, 1)
                dve.wait_ge(end_step, n0 + 2)
                dve.tensor_reduce(norm[:, 0:1], res[:, :], AX.X, ALU.add).then_inc(end_step, 1)
                dve.wait_ge(end_step, n0 + 3)
                dve.tensor_scalar(norm[:, 1:2], norm[:, 0:1], 1.0 / C, None, ALU.mult).then_inc(end_step, 1)
                dve.wait_ge(end_step, n0 + 4)
                dve.tensor_scalar(cen[:, :], res[:, :], norm[:, 1:2], None, ALU.subtract).then_inc(end_step, 1)

            def normalise(s):
                dve.wait_ge(end_std, s + 1)
                dve.reciprocal(norm[:, 4:5], norm[:, 3:4]).then_inc(end_step, 1)
                dve.wait_ge(y_out, s * 16 + CREDIT_DMA)
                dve.wait_ge(end_step, s * ND + 2 * ND)
                dve.tensor_scalar(y[:, :], cen[:, :], norm[:, 4:5], None, ALU.mult).then_inc(y_ready, 1)

            dve.wait_ge(src_first, 16)
            dve.tensor_copy(src_f[:, 0, :], src_t[:, 0, :]).then_inc(src_f_ready, 1)
            dve.wait_ge(src_ps, 1)
            for u in range(2):
                dve.tensor_copy(ix[u][:, :], ps_src[0][:, u * ST:(u + 1) * ST]).then_inc(ix_copied, SG)
            chain(dve.memset(dst_r[:, :], N))
            dve.memset(dst_r[0:1, 0:1], -1).then_inc(pads_ready, 2)
            dve.memset(first_dst[:, :], N - 1).then_inc(pads_ready, 1)
            dve.memset(runmax[:, 1, GE - 1:GE], SCALE)
            dve.memset(ones[:, :], 1.0).then_inc(ones_ready, 1)
            dve.memset(rows[:, :, :, C:C1], 1.0).then_inc(ones_ready, 1)
            dve.memset(eps_col[:, :], EPS).then_inc(ones_ready, 1)
            dve.memset(acc[:, :], 0.0).then_inc(ones_ready, 1)
            dve.sem_inc(g_merged, 1)
            dve.tensor_copy(src_ix[:, 0:P], ps_src[0]).then_inc(src_ix_ready, 1)
            if FULL_T // P > 1:
                dve.wait_ge(src_in, 16)
            dve.wait_ge(src_pad_in, 32 if REST else 16)
            dve.tensor_copy(src_f[:, 1:TB, :], src_t[:, 1:TB, :]).then_inc(src_f_ready, 1)
            for b in range(1, TB):
                dve.wait_ge(src_ps, b + 1)
                dve.tensor_copy(src_ix[:, b * P:(b + 1) * P], ps_src[b % 4]).then_inc(src_ix_ready, 1)
            dve.wait_ge(dst_in, 64 if SMID else 48)
            chain(dve.tensor_scalar(win_col[:, :], dst_r[:, 1:2], float(N - P), -1.0, ALU.min, ALU.add))
            chain(dve.memset(win_col[0:1, :], -1.0))
            dve.tensor_scalar(keys[:, :], dst_r[:, 0:SE + 1], win_col[:, :], SCALE, ALU.subtract, ALU.mult).then_inc(keys_ready, 1)
            chain(dve.tensor_tensor(step[:, :], dst_r[:, 1:SE + 2], dst_r[:, 0:SE + 1], ALU.subtract))
            dve.tensor_reduce(order_col[:, :], step[:, :], AX.X, ALU.min).then_inc(order_ready, 1)
            dve.wait_ge(win_in, 16)
            chain(dve.tensor_scalar(win0[:, :], first_dst[:, :], float(N - P), None, ALU.min))
            chain(dve.memset(win0[:, 0:1], 0))
            dve.memset(moved[:, 0:1], 0.0).then_inc(moved_ready, 1)
            dve.tensor_tensor(moved[:, 1:NSB], win0[:, 1:NSB], win0[:, 0:NSB - 1], ALU.subtract).then_inc(moved_ready, 1)
            chain(dve.tensor_tensor(win_step[:, :], first_dst[:, 1:NSB + 1], win0[:, 0:NSB], ALU.subtract))
            chain(dve.tensor_reduce(order[:, 0:1], win_step[:, :], AX.X, ALU.max))
            chain(dve.tensor_scalar(order[:, 1:2], order[:, 0:1], -1.0, float(P - 1), ALU.mult, ALU.add))
            dve.wait_ge(order_ps, 1)
            chain(dve.tensor_reduce(order[:, 2:3], ps_order, AX.X, ALU.min))
            chain(dve.tensor_tensor(order[:, 3:4], order[:, 1:2], order[:, 2:3], ALU.min))
            dve.tensor_scalar(in_order[:, :], order[:, 3:4], 0.0, None, ALU.is_ge).then_inc(flag_ready, 1)
            dve.wait_ge(consts_ready, 4)
            dve.tensor_scalar(slot_key[:, :], slot_col[:, :], SCALE, None, ALU.mult).then_inc(slot_keys_ready, 1)
            dve.tensor_scalar(slot_keys[:, :], slot_row[:, :], SCALE, None, ALU.mult).then_inc(slot_keys_ready, 1)
            dve.wait_ge(moved_ps, 1)
            dve.tensor_scalar(carry_col[:, :], ps_moved, -1.0, slot_col[:, :], ALU.mult, ALU.add).then_inc(carry_ready, 1)
            dve.wait_ge(x_in, 16)
            dve.tensor_reduce(part[0:PN, :], xn[0:PN, :, :].rearrange("p t c -> p c t"), AX.X, ALU.add).then_inc(part_ready, 1)
            dve.wait_ge(sum_ps, 1)
            chain(dve.tensor_scalar(mean_b[:, :], ps_sum, 1.0 / N, None, ALU.mult))
            dve.tensor_tensor(xc[0:PN, :, :], xn[0:PN, :, :],
                              mean_b[0:PN, :].rearrange("p (a c) -> p a c", a=1).to_broadcast([PN, TN, C]),
                              ALU.subtract).then_inc(xc_ready, 1)
            dve.scalar_tensor_tensor(last_r[:, :], step[:, 1:SE + 1], 0.0, keys[:, 1:SE + 1], ALU.is_gt, ALU.mult).then_inc(last_r_ready, 1)
            dve.wait_ge(sq_ready, 1)
            dve.tensor_reduce(part_sq[0:PN, :], xc[0:PN, :, :].rearrange("p t c -> p c t"), AX.X, ALU.add).then_inc(part_ready, 1)
            dve.wait_ge(var_ps, 1)
            dve.tensor_scalar(bn[:, 1:2], ps_var[:, 0:1], 1.0 / N, EPS, ALU.mult, ALU.add).then_inc(std_in, 1)
            chain(dve.tensor_scalar(bn[:, 0:1], ps_var[:, 1:2], 1.0 / N, None, ALU.mult))
            dve.wait_ge(std_ready, 1)
            dve.wait_ge(par_in, 160)
            chain(dve.reciprocal(bn[:, 3:4], bn[:, 2:3]))
            chain(dve.tensor_tensor(bn[:, 4:5], bn[:, 3:4], gam[:, :], ALU.mult))
            chain(dve.tensor_tensor(bn[:, 3:4], bn[:, 0:1], bn[:, 4:5], ALU.mult))
            chain(dve.tensor_tensor(bn[:, 5:6], bet[:, :], bn[:, 3:4], ALU.subtract))
            chain(dve.tensor_tensor(w_raw[C:2 * C, :], w_a[C:2 * C, :], w_raw[C:2 * C, :], ALU.subtract))
            dve.tensor_scalar(w_cat[:, :], w_raw[:, :], bn[:, 4:5], None, ALU.mult).then_inc(fold_ready, 1)
            dve.wait_ge(bias_ps, 1)
            dve.tensor_tensor(bias1[:, :], ps_bias, b1c[:, :], ALU.add).then_inc(weights_ready, 1)
            dve.wait_ge(slot_keys_ready, 2)
            dve.wait_ge(carry_ready, 1)
            dve.wait_ge(last_ready, len(LAST_CUTS))
            dve.wait_ge(flag_ready, 1)
            windowed = dve.value_load(in_order[0:1, 0:1], min_val=0, max_val=1)
            with dve.If(windowed == 1):
                with dve.Fori(0, ITERS) as it:
                    base = it * IG
                    for k in range(IG + 6):
                        if k < IG:
                            u, g = divmod(k, SG)
                            e0 = KB0 + g * GE
                            if g == 0:
                                n0 = u * 4
                                dve.wait_ge(xwin_in[u], it * 16 + 16)
                                dve.tensor_copy(xw[u][:, 0, :], xwin[u][:, :]).then_inc(split_step, 1)
                                dve.wait_ge(split_step, it * 8 + (n0 + 1))
                                dve.tensor_tensor(xw_rest[:, :], xwin[u][:, :], xw[u][:, 0, :], ALU.subtract).then_inc(split_step, 1)
                                dve.wait_ge(split_step, it * 8 + (n0 + 2))
                                dve.tensor_copy(xw[u][:, 1, :], xw_rest[:, :]).then_inc(split_step, 1)
                                dve.wait_ge(split_step, it * 8 + (n0 + 3))
                                dve.tensor_tensor(xw[u][:, 2, :], xw_rest[:, :], xw[u][:, 1, :], ALU.subtract).then_inc(split_step, 1)
                                dve.wait_ge(key_in[u], it * 16 + 16)
                            if k >= 2:
                                dve.wait_ge(feat_ps, base + (IG + k - 1))
                            dve.tensor_scalar(onehot[:, k % 2, :], kb[u][:, e0:e0 + GE], slot_key[:, :], None,
                                              ALU.is_equal).then_inc(onehot_ready, 1)
                            dve.tensor_tensor(reset[:, g, :], kb[u][0:C, e0:e0 + GE], kb[u][0:C, e0 - 1:e0 - 1 + GE],
                                              ALU.subtract).then_inc(reset_ready, 1)
                        j = k - 3
                        if 0 <= j < IG:
                            dve.wait_ge(msg_ps, base + (j + 1))
                            dve.wait_ge(reset_ready, base + (j + 1))
                            if j >= 2:
                                dve.wait_ge(rows_ps, base + (j - 1))
                            if j > 0:
                                dve.wait_ge(run_ready, base + j)
                            dve.tensor_tensor_scan(runmax[:, j % 2, :], reset[:, j % SG, :], ps_msg[0:C, j % 2, :],
                                                   runmax[:, (j + 1) % 2, GE - 1:GE], ALU.add, ALU.max).then_inc(run_ready, 1)
                        j = k - 4
                        if 0 <= j < IG:
                            u, g = divmod(j, SG)
                            if j >= 2:
                                dve.wait_ge(acc_ps, base + (j - 1))
                            if g == 0:
                                dve.tensor_tensor(shift[:, :], slot_row[:, :], carry_col[:, bass.ds(it * 2 + u, 1)].to_broadcast([P, P]),
                                                  ALU.is_equal).then_inc(shift_ready, 1)
                            dve.tensor_tensor(pick[:, j % 2, :, :],
                                              slot_keys[:, :].rearrange("p (a n) -> p a n", a=1).to_broadcast([P, TG, P]),
                                              last_key[:, g * TG:(g + 1) * TG, bass.ds(it * 2 + u, 1)].to_broadcast([P, TG, P]),
                                              ALU.is_equal).then_inc(pick_ready, 1)
                        if k in AT_CENTRE:
                            u = AT_CENTRE.index(k)
                            centre(it * 2 + u, u, it + 1)
                        if k in AT_NORM:
                            normalise(it * 2 + AT_NORM.index(k))
            with dve.Else():
                dve.memset(best[0:C, :], SCALE).then_inc(g_msg, 1)
                dve.memset(best[C:C1, :], 0.0).then_inc(g_msg, 1)
                dve.memset(msg[C:C1, :], 1.0).then_inc(g_msg, 1)
                with dve.Fori(0, GT) as i:
                    dve.wait_ge(g_dst_in, i * 32 + 32)
                    dve.wait_ge(g_msg_ps, i + 1)
                    dve.tensor_copy(msg[0:C, :], ps_msg[0:C, 0, 0:P]).then_inc(g_msg, 1)
                    with dve.Fori(0, P) as e:
                        node = dve.value_load(dst_row[0:1, bass.ds(e, 1)], min_val=0, max_val=N)
                        dve.wait_ge(g_msg, i + 4)
                        dve.wait_ge(g_merged, i * P + e + 1)
                        dve.tensor_tensor(best[:, bass.ds(node, 1)], best[:, bass.ds(node, 1)], msg[:, bass.ds(e, 1)],
                                          ALU.max).then_inc(g_merged, 1)

                def node_block(b, first):
                    dve.wait_ge(g_merged, GT * P + 1)
                    dve.tensor_copy(msg[:, :], best[:, bass.ds(first, P)]).then_inc(g_block, 1)
                    centre(b, 0, b + 1)
                    normalise(b)

                node_blocks(dve, node_block)

        @block.tensor
        def _(pe):
            pe.sem_inc(feat_ps, IG)
            pe.wait_ge(consts_ready, 4)
            for b in range(TB):
                pe.wait_ge(src_f_ready, 1 if b == 0 else 2)
                if b >= 4:
                    pe.wait_ge(src_ix_ready, b - 3)
                pe.transpose(ps_src[b % 4], src_f[:, b, :], ident[:, :]).then_inc(src_ps, 1)
            pe.wait_ge(order_ready, 1)
            pe.transpose(ps_order, order_col[:, :], ident[0:NSB, 0:NSB]).then_inc(order_ps, 1)
            pe.wait_ge(ones_ready, 1)
            pe.wait_ge(moved_ready, 2)
            pe.matmul(ps_moved, ones[0:1, :], moved[:, :], start=True, stop=True).then_inc(moved_ps, 1)
            pe.wait_ge(part_ready, 1)
            pe.matmul(ps_sum, ones[0:PN, :], part[0:PN, :], start=True, stop=True).then_inc(sum_ps, 1)
            pe.wait_ge(src_ix_ready, TB)
            pe.wait_ge(last_r_ready, 1)
            for b, t0, t1 in LAST_CUTS:
                for t in range(t0, t1):
                    last = pe.transpose(ps_last[b][:, (t - t0) * NSB:(t - t0 + 1) * NSB], last_r[:, t * P:(t + 1) * P],
                                        ident[0:NSB, 0:NSB])
                last.then_inc(last_ps, 1)
            pe.wait_ge(part_ready, 2)
            for col, of in ((0, part_sq), (1, part)):
                for h in range(2):
                    last = pe.matmul(ps_var[h * C:(h + 1) * C, col:col + 1], of[0:PN, :], ones[0:PN, 0:1], start=True, stop=True)
            last.then_inc(var_ps, 1)
            pe.wait_ge(carry_ready, 1)
            pe.wait_ge(fold_ready, 1)
            pe.matmul(ps_bias, w_raw[:, :], bn[:, 5:6], start=True, stop=True).then_inc(bias_ps, 1)
            pe.wait_ge(weights_ready, 1)
            pe.wait_ge(last_ready, len(LAST_CUTS))
            pe.wait_ge(flag_ready, 1)
            windowed = pe.value_load(in_order[0:1, 0:1], min_val=0, max_val=1)
            with pe.If(windowed == 1):
                with pe.Fori(0, ITERS) as it:
                    base = it * IG
                    for k in range(IG + 5):
                        if k < IG:
                            u, g = divmod(k, SG)
                            if k >= 2:
                                pe.wait_ge(feat_sb, base + (k - 1))
                            pe.wait_ge(rows_in[k], it * (16 * TG) + 16 * TG)
                            if g == 0:
                                pe.wait_ge(split_step, it * 8 + 4 * (u + 1))
                            pe.wait_ge(onehot_ready, base + (k + 1))
                            for w in range(3):
                                pe.matmul(ps_feat[C:2 * C, k % 2, :], xw[u][:, w, :], onehot[:, k % 2, :], start=(w == 0), stop=(w == 2))
                            for t in range(TG):
                                last = pe.transpose(ps_feat[0:C, k % 2, t * P:(t + 1) * P], xs[:, k, t, :], ident[:, :])
                            last.then_inc(feat_ps, 1)
                        j = k - 1
                        if 0 <= j < IG:
                            pe.wait_ge(feat_sb, base + (j + 1))
                            if j >= 2:
                                pe.wait_ge(hid_sb, base + (j - 1))
                            pe.matmul(ps_hid[:, j % 2, :], w_cat[:, :], feat[:, j % 2, :], start=True, stop=True).then_inc(hid_ps, 1)
                        j = k - 2
                        if 0 <= j < IG:
                            pe.wait_ge(hid_sb, base + (j + 1))
                            if j >= 2:
                                pe.wait_ge(run_ready, base + (j - 1))
                            pe.matmul(ps_msg[0:C, j % 2, :], w2[:, :], hid[:, j % 2, :], start=True, stop=True).then_inc(msg_ps, 1)
                        j = k - 5
                        if 0 <= j < IG:
                            u, g = divmod(j, SG)
                            pe.wait_ge(rows_sb, base + (j + 1))
                            pe.wait_ge(pick_ready, base + (j + 1))
                            if g == 0:
                                pe.wait_ge(acc_sb, it * 2 + (u + 1))
                                pe.wait_ge(shift_ready, it * 2 + (u + 1))
                                pe.matmul(ps_acc[:, 0:C1], shift[:, :], acc[:, :], start=True, stop=False)
                            for t in range(TG):
                                last = pe.matmul(ps_acc[:, 0:C1], pick[:, j % 2, t, :], rows[:, j % 2, t, :],
                                                 start=False, stop=(g == SG - 1 and t == TG - 1))
                            last.then_inc(acc_ps, 1)
                        j = k - 4
                        if 0 <= j < IG:
                            pe.wait_ge(consts_ready, 4)
                            pe.wait_ge(run_ready, base + (j + 1))
                            for t in range(TG):
                                last = pe.transpose(ps_rows[:, t * C:(t + 1) * C], runmax[:, j % 2, t * P:(t + 1) * P], ident[0:C, 0:C])
                            last.then_inc(rows_ps, 1)
            with pe.Else():
                with pe.Fori(0, GT) as i:
                    pe.wait_ge(g_pair_in, i * 32 + 32)
                    pe.transpose(ps_feat[:, 0, 0:P], pair[:, :, :].rearrange("p s c -> p (s c)"), ident[:, :]).then_inc(g_feat_ps, 1)
                    pe.wait_ge(g_feat, i + 1)
                    pe.matmul(ps_hid[:, 0, 0:P], w_cat[:, :], feat[:, 0, 0:P], start=True, stop=True).then_inc(g_hid_ps, 1)
                    pe.wait_ge(g_hid, i + 1)
                    pe.matmul(ps_msg[0:C, 0, 0:P], w2[:, :], hid[:, 0, 0:P], start=True, stop=True).then_inc(g_msg_ps, 1)

                def node_block(b, first):
                    pe.wait_ge(consts_ready, 4)
                    pe.wait_ge(acc_sb, b + 1)
                    pe.wait_ge(g_block, b + 1)
                    pe.transpose(ps_acc[:, 0:C1], msg[:, :], ident[0:C1, 0:C1]).then_inc(acc_ps, SG)

                node_blocks(pe, node_block)



_INS = ["x", "src", "dst", "L0_gnn_gamma", "L0_gnn_beta", "L0_gnn_W1", "L0_gnn_b1", "L0_gnn_W2", "L0_gnn_b2"]


def kernel(**inputs):
    import concourse.bacc as bacc
    from concourse.bass_utils import run_bass_kernel_spmd as run

    nc = bacc.Bacc("TRN2", target_bir_lowering=False, num_devices=1)
    arrays, args = {}, []
    for name in _INS:
        a = np.ascontiguousarray(inputs[name])
        arrays[f"in_{name}"] = a
        args.append(nc.dram_tensor(f"in_{name}", a.shape, mybir.dt.from_np(a.dtype), kind="ExternalInput").ap())
    out = nc.dram_tensor("out_0", inputs["x"].shape, mybir.dt.float32, kind="ExternalOutput").ap()
    edge_conv_program(nc, *args, out)
    r = run(nc, [arrays], core_ids=[0])
    return r.results[0]["out_0"]
```

```python
import concourse.bass as bass
import concourse.mybir as mybir
import numpy as np
from contextlib import ExitStack


def edge_conv_program(nc, x, src, dst, gamma, beta, W1, b1, W2, b2, out):
    f32, i32, bf16 = mybir.dt.float32, mybir.dt.int32, mybir.dt.bfloat16
    ALU, ACT, AX = mybir.AluOpType, mybir.ActivationFunctionType, mybir.AxisListType

    P = 128
    N, C = x.shape
    E = src.shape[0]
    HID = W1.shape[1]
    TG = 4
    GE = TG * P
    SG = 7
    ST = SG * TG
    SE = SG * GE
    NSB = -(-E // (2 * SE)) * 2
    ITERS, IG = NSB // 2, 2 * SG
    EP = NSB * SE
    PAD = EP - E
    TILES = EP // P
    GT0, GT = PAD // P, -(-E // P)
    TB = -(-TILES // P)
    PART = PAD % P
    FIRST = -(-PAD // P)
    SKIP = [t for t in range(PAD // P) if t % TG < TG - 1]
    PN = max(p for p in range(1, P + 1) if N % p == 0)
    TN = N // PN
    C1 = C + 1
    SMID = (NSB - 2) // 16 * 16
    SCALE = -(2.0 ** 112)
    EPS = 1e-5
    CREDIT_DMA = 16
    AT_ACC, AT_CENTRE, AT_STD, AT_NORM = [SG + 1, IG + 1], [SG + 3, IG + 1], [SG + 3, IG + 1], [SG + 4, IG + 1]
    GATHER_CUTS = [(0, SG // 3), (SG // 3, 2 * SG // 3), (2 * SG // 3, SG)]
    ROWS0 = [16 * (TG - sum(t // TG == k for t in SKIP)) for k in range(IG)]
    ND = 6
    KT = GE // NSB
    assert N >= P and PAD + 1 < SE and TILES > P >= 2 * ST and -(-ST // KT) <= 4

    keys_dram = nc.dram_tensor("keys_dram", [NSB, SE + 1], bf16, kind="Internal").ap()
    dst_dram = nc.dram_tensor("dst_dram", [EP], i32, kind="Internal").ap()

    ctx = ExitStack()
    with ctx:
        def sb(name, shape, dt=f32):
            return ctx.enter_context(nc.sbuf_tensor(name, shape, dt))

        def pb(name, shape, dt=f32):
            return ctx.enter_context(nc.psum_tensor(name, shape, dt))

        def sem(name):
            return ctx.enter_context(nc.semaphore(name))

        ident = sb("ident", [P, P])
        ones = sb("ones", [P, P])
        eps_col = sb("eps_col", [P, 1])
        slot_col = sb("slot_col", [P, 1])
        slot_row = sb("slot_row", [P, P])
        src_t = sb("src_t", [P, TB, P], i32)
        src_f = sb("src_f", [P, TB, P])
        src_ix = sb("src_ix", [P, TB * P], i32)
        dst_r = sb("dst_r", [NSB, SE + 2], i32)
        win_col = sb("win_col", [NSB, 1])
        keys = sb("keys", [NSB, SE + 1], bf16)
        step = sb("step", [NSB, SE + 1], bf16)
        last_r = sb("last_r", [NSB, SE])
        last_key = sb("last_key", [P, ST, NSB])
        first_dst = sb("first_dst", [1, NSB + 1], i32)
        win0 = sb("win0", [1, NSB + 1], i32)
        win_step = sb("win_step", [1, NSB])
        moved = sb("moved", [1, NSB])
        carry_col = sb("carry_col", [P, NSB])
        slot_key = sb("slot_key", [P, 1])
        slot_keys = sb("slot_keys", [P, P])
        down = sb("down", [NSB, SE + 1], bf16)
        order_col = sb("order_col", [NSB, 1])
        order = sb("order", [1, 4])
        in_order = sb("in_order", [1, 1], i32)
        xn = sb("xn", [P, TN, C])
        xc = sb("xc", [P, TN, C])
        part = sb("part", [P, C])
        part_sq = sb("part_sq", [P, C])
        mean_b = sb("mean_b", [P, C])
        w_raw = sb("w_raw", [P, HID])
        w_a = sb("w_a", [P, HID])
        w_cat = sb("w_cat", [P, HID])
        w2 = sb("w2", [HID, C])
        b1c = sb("b1c", [HID, 1])
        bias1 = sb("bias1", [HID, 1])
        b2b = sb("b2b", [P, C])
        gam = sb("gam", [P, 1])
        bet = sb("bet", [P, 1])
        bn = sb("bn", [P, 6])
        ix = [sb(f"ix{u}", [P, ST], i32) for u in range(2)]
        xs = sb("xs", [P, IG, TG, C])
        KB0 = 16
        kb = [sb(f"kb{u}", [P, KB0 + SE], bf16) for u in range(2)]
        xwin = [sb(f"xwin{u}", [P, C]) for u in range(2)]
        xw = [sb(f"xw{u}", [P, 3, C], bf16) for u in range(2)]
        xw_rest = sb("xw_rest", [P, C])
        onehot = sb("onehot", [P, 2, GE], bf16)
        reset = sb("reset", [C, SG, GE], bf16)
        feat = sb("feat", [P, 2, GE])
        hid = sb("hid", [HID, 2, GE])
        runmax = sb("runmax", [C, 2, GE])
        rows = sb("rows", [P, 2, TG, C1])
        pick = sb("pick", [P, 2, TG, P])
        shift = sb("shift", [P, P])
        acc = sb("acc", [P, C1])
        res = sb("res", [P, C])
        cen = sb("cen", [P, C])
        cen_sq = sb("cen_sq", [P, C])
        norm = sb("norm", [P, 5])
        y = sb("y", [P, C])
        best = sb("best", [C1, 1 + N])
        pair_dst = sb("pair_dst", [P, 1], i32)
        pair_ix = sb("pair_ix", [P, 2], i32)
        pair = sb("pair", [P, 2, C])
        dst_row = sb("dst_row", [1, P], i32)
        col_row = sb("col_row", [1, P], i32)
        msg = sb("msg", [C1, P])

        ps_feat = pb("ps_feat", [P, 2, GE])
        ps_hid = pb("ps_hid", [HID, 2, GE])
        ps_msg = pb("ps_msg", [P, 2, GE])
        ps_rows = pb("ps_rows", [P, GE])
        ps_acc = pb("ps_acc", [P, GE])
        ps_src = [ps_feat[:, 0, 0:P], ps_feat[:, 1, 0:P], ps_hid[:, 0, 0:P], ps_hid[:, 1, 0:P]]
        ps_last = [ps_feat[:, 0, :], ps_feat[:, 1, :], ps_hid[:, 0, :], ps_hid[:, 1, :]]
        ps_order = ps_msg[0:1, 0, 0:1]
        ps_sum = ps_msg[:, 1, 0:C]
        ps_var = ps_rows[:, 0:2]
        ps_moved = ps_acc[:, 0:NSB]
        ps_bias = ps_acc[:, 0:1]
        LAST_CUTS = [(b, b * KT, min(ST, (b + 1) * KT)) for b in range(-(-ST // KT))]

        consts_ready = sem("consts_ready")
        ones_ready = sem("ones_ready")
        skip_ready = sem("skip_ready")
        src_pad_ready, pads_ready = sem("src_pad_ready"), sem("pads_ready")
        src_first, src_in = sem("src_first"), sem("src_in")
        dst_in, x_in, win_in, par_in = sem("dst_in"), sem("x_in"), sem("win_in"), sem("par_in")
        keys_out = sem("keys_out")
        src_f_ready, src_ps, src_ix_ready = sem("src_f_ready"), sem("src_ps"), sem("src_ix_ready")
        keys_ready, step_ready = sem("keys_ready"), sem("step_ready")
        last_r_ready, last_ps, last_ready = sem("last_r_ready"), sem("last_ps"), sem("last_ready")
        g_dst_out, g_dst_in, g_ix, g_pair_in = sem("g_dst_out"), sem("g_dst_in"), sem("g_ix"), sem("g_pair_in")
        g_feat_ps, g_feat, g_hid_ps, g_hid = sem("g_feat_ps"), sem("g_feat"), sem("g_hid_ps"), sem("g_hid")
        g_msg_ps, g_msg, g_merged = sem("g_msg_ps"), sem("g_msg"), sem("g_merged")
        g_block, g_col = sem("g_block"), sem("g_col")
        order_ready, order_ps, flag_ready = sem("order_ready"), sem("order_ps"), sem("flag_ready")
        part_ready, sum_ps, xc_ready, sq_ready, var_ps = sem("part_ready"), sem("sum_ps"), sem("xc_ready"), sem("sq_ready"), sem("var_ps")
        std_in, std_ready = sem("std_in"), sem("std_ready")
        fold_ready, bias_ps, weights_ready = sem("fold_ready"), sem("bias_ps"), sem("weights_ready")
        slot_keys_ready = sem("slot_keys_ready")
        dve_step = sem("dve_step")
        ix_first = sem("ix_first")
        ix_in = [sem(f"ix_in{u}") for u in range(2)]
        rows_in = [sem(f"rows_in{k}") for k in range(IG)]
        key_in = [sem(f"key_in{u}") for u in range(2)]
        xwin_in = [sem(f"xwin_in{u}") for u in range(2)]
        split_step = sem("split_step")
        onehot_ready, reset_ready = sem("onehot_ready"), sem("reset_ready")
        feat_ps, feat_sb = sem("feat_ps"), sem("feat_sb")
        hid_ps, hid_sb = sem("hid_ps"), sem("hid_sb")
        msg_ps, run_ready = sem("msg_ps"), sem("run_ready")
        rows_ps, rows_sb, pick_ready = sem("rows_ps"), sem("rows_sb"), sem("pick_ready")
        moved_ready, moved_ps, carry_ready, shift_ready = sem("moved_ready"), sem("moved_ps"), sem("carry_ready"), sem("shift_ready")
        acc_ps, acc_sb = sem("acc_ps"), sem("acc_sb")
        end_step, end_sq, end_std, y_ready, y_out = sem("end_step"), sem("end_sq"), sem("end_std"), sem("y_ready"), sem("y_out")

        block = ctx.enter_context(nc.Block())

        def overlapped(ap, start, rows_, width, stride):
            return bass.AP(tensor=ap.tensor, offset=start, ap=[[stride, rows_], [1, width]])

        def node_blocks(eng, body):
            with eng.Fori(0, N // P) as b:
                body(b, b * P)
            if N % P:
                body(N // P, N - P)

        @block.sync
        def _(sp):
            def edge(tile):
                return tile * P - PAD

            sp.dma_start(src_t[FIRST:P, 0, :], src[edge(FIRST):edge(P)].rearrange("(t i) -> t i", i=P)).then_inc(src_first, 16)
            sp.wait_ge(src_pad_ready, 1 + (FIRST > 0))
            if PART:
                sp.dma_start(src_t[FIRST - 1:FIRST, 0, PART:P], src[0:P - PART].rearrange("(t i) -> t i", t=1)).then_inc(src_first, 16)
            whole = TILES // P
            if whole > 1:
                sp.dma_start(src_t[:, 1:whole, :],
                             src[edge(P):edge(whole * P)].rearrange("(b t i) -> t b i", t=P, i=P)).then_inc(src_in, 16)
            if TILES % P:
                sp.dma_start(src_t[0:TILES % P, whole, :], src[edge(whole * P):E].rearrange("(t i) -> t i", i=P)).then_inc(src_in, 16)
            sp.wait_ge(pads_ready, 2)
            sp.dma_start(dst_r[0:1, 1 + PAD:SE + 2], overlapped(dst, 0, 1, SE + 1 - PAD, SE)).then_inc(dst_in, 16)
            if SMID:
                sp.dma_start(dst_r[1:1 + SMID, :], overlapped(dst, SE - PAD - 1, SMID, SE + 2, SE)).then_inc(dst_in, 16)
            sp.dma_start(dst_r[1 + SMID:NSB - 1, :],
                         overlapped(dst, (1 + SMID) * SE - PAD - 1, NSB - 2 - SMID, SE + 2, SE)).then_inc(dst_in, 16)
            sp.dma_start(dst_r[NSB - 1:NSB, 0:SE + 1], overlapped(dst, E - SE - 1, 1, SE + 1, SE)).then_inc(dst_in, 16)
            sp.dma_start(xn[0:PN, :, :], x.rearrange("(p t) c -> p t c", t=TN)).then_inc(x_in, 16)
            sp.wait_ge(keys_ready, 1)
            sp.dma_start(keys_dram, keys[:, :]).then_inc(keys_out, 16)
            sp.wait_ge(keys_out, 16)
            sp.wait_ge(src_ix_ready, TB)
            sp.wait_ge(flag_ready, 1)
            windowed = sp.value_load(in_order[0:1, 0:1], min_val=0, max_val=1)

            def load_keys(s, u):
                sp.dma_start(kb[u][:, KB0 - 1:KB0 + SE],
                             keys_dram[bass.ds(s, 1), :].to_broadcast([P, SE + 1])).then_inc(key_in[u], 16)

            def load_window(s, u):
                first = sp.value_load(win0[0:1, bass.ds(s, 1)], min_val=0, max_val=N - P)
                sp.dma_start(xwin[u][:, :], x[bass.ds(first, P), :]).then_inc(xwin_in[u], 16)

            def store_window(s):
                first = sp.value_load(win0[0:1, bass.ds(s, 1)], min_val=0, max_val=N - P)
                sp.wait_ge(y_ready, s + 1)
                sp.dma_start(out[bass.ds(first, P), :], y[:, :]).then_inc(y_out, 16)

            with sp.If(windowed == 1):
                for u in range(2):
                    load_keys(u, u)
                    load_window(u, u)
                with sp.Fori(0, ITERS - 1) as it:
                    for u in range(2):
                        arrived = {n: sp.to_reg(it * (16 * TG) + n) for n in sorted(set(ROWS0[u * SG:(u + 1) * SG]))}
                        for g in range(SG):
                            sp.wait_ge(rows_in[u * SG + g], arrived[ROWS0[u * SG + g]])
                        sp.dma_start(ix[u][:, :], src_ix[:, bass.ds(it * (2 * ST) + (2 + u) * ST, ST)]).then_inc(ix_in[u], 16)
                        sp.wait_ge(reset_ready, it * IG + SG * (u + 1))
                        load_keys(it * 2 + (2 + u), u)
                        sp.wait_ge(end_step, it * (2 * ND) + (ND * (u + 1) + 2))
                        load_window(it * 2 + (2 + u), u)
                        store_window(it * 2 + u)
                for u in range(2):
                    store_window(NSB - 2 + u)
                sp.wait_ge(y_out, CREDIT_DMA + 16 * NSB)
            with sp.Else():
                sp.dma_start(dst_dram.rearrange("(s e) -> s e", e=SE), dst_r[:, 1:SE + 1]).then_inc(g_dst_out, 16)

                def node_block(b, first):
                    sp.wait_ge(end_step, b * ND + 2)
                    sp.dma_start(xwin[0][:, :], x[bass.ds(first, P), :]).then_inc(xwin_in[0], 16)
                    sp.wait_ge(y_ready, b + 1)
                    sp.dma_start(out[bass.ds(first, P), :], y[:, :]).then_inc(y_out, 16)

                node_blocks(sp, node_block)
                sp.wait_ge(y_out, CREDIT_DMA + 16 * -(-N // P))

        @block.gpsimd
        def _(pool):
            if FIRST:
                pool.memset(src_t[0:FIRST, 0, :], 0).then_inc(src_pad_ready, 1)
            pool.memset(src_t[:, TB - 1, :], 0).then_inc(src_pad_ready, 1)
            pool.memset(ident[:, :], 0.0).then_inc(consts_ready, 1)
            pool.wait_ge(consts_ready, 1)
            pool.affine_select(out=ident[:, :], in_=ident[:, :], compare_op=ALU.not_equal, fill=1.0, base=0,
                               pattern=[[-1, P]], channel_multiplier=1).then_inc(consts_ready, 1)
            pool.iota(slot_col[:, :], pattern=[[0, 1]], base=1, channel_multiplier=1,
                      allow_small_or_imprecise_dtypes=True).then_inc(consts_ready, 1)
            pool.iota(slot_row[:, :], pattern=[[1, P]], base=1, channel_multiplier=0,
                      allow_small_or_imprecise_dtypes=True).then_inc(consts_ready, 1)

            def gather(it):
                later = not isinstance(it, int)
                for u in range(2):
                    for g0, g1 in GATHER_CUTS:
                        used = u * SG + g1
                        if later:
                            used = pool.to_reg(it * IG + used)
                            copied = pool.to_reg(it * 16)
                        pool.wait_ge(ix_first, 2)
                        pool.wait_ge(feat_ps, used)
                        if later:
                            pool.wait_ge(ix_in[u], copied)
                        for g in range(g0, g1):
                            for t in range(TG):
                                col = g * TG + t
                                if not later and u * ST + col in SKIP:
                                    continue
                                pool.indirect_dma_start(xs[:, u * SG + g, t, :], None, x[:, :],
                                                        bass.IndirectOffsetOnAxis(ap=ix[u][:, col:col + 1], axis=0))\
                                    .then_inc(rows_in[u * SG + g], 16)

            gather(0)
            pool.wait_ge(flag_ready, 1)
            windowed = pool.value_load(in_order[0:1, 0:1], min_val=0, max_val=1)
            with pool.If(windowed == 1):
                with pool.Fori(1, ITERS) as it:
                    gather(it)
            with pool.Else():
                with pool.Fori(0, GT) as i:
                    pool.wait_ge(g_dst_in, i * 32 + 32)
                    pool.wait_ge(g_merged, i * P + 1)
                    pool.tensor_copy(pair_ix[:, 0:1], src_ix[:, bass.ds(i + GT0, 1)]).then_inc(g_ix, 16)
                    pool.tensor_scalar(pair_ix[:, 1:2], pair_dst[:, :], 0.0, 0.0, ALU.add, ALU.max).then_inc(g_ix, 16)
                    pool.wait_ge(src_ix_ready, TB)
                    pool.wait_ge(g_ix, i * 32 + 32)
                    for side in range(2):
                        pool.indirect_dma_start(pair[:, side, :], None, x[:, :],
                                                bass.IndirectOffsetOnAxis(ap=pair_ix[:, side:side + 1], axis=0)).then_inc(g_pair_in, 16)

        @block.scalar
        def _(act):
            def take_acc(s):
                act.wait_ge(acc_ps, s * SG + SG)
                act.wait_ge(end_step, s * ND + 1)
                act.activation(acc[:, :], ps_acc[:, 0:C1], ACT.Copy).then_inc(acc_sb, 1)

            def deviation(s):
                act.wait_ge(end_step, s * ND + (ND + 5))
                act.activation(cen_sq[:, :], cen[:, :], ACT.Square, accum_out=norm[:, 2:3]).then_inc(end_sq, 1)
                act.wait_ge(end_sq, s + 1)
                act.activation(norm[:, 3:4], norm[:, 2:3], ACT.Sqrt, bias=eps_col[:, :], scale=1.0 / C).then_inc(end_std, 1)

            act.wait_ge(pads_ready, 3)
            act.dma_start(first_dst[:, 1:NSB], bass.AP(tensor=dst.tensor, offset=SE - PAD, ap=[[0, 1], [SE, NSB - 1], [1, 1]]),
                          allow_slow_non_contiguous=True).then_inc(win_in, 16)
            for h in range(2):
                act.dma_start(w_raw[h * C:(h + 1) * C, :], W1[C:2 * C, :]).then_inc(par_in, 16)
                act.dma_start(gam[h * C:(h + 1) * C, :], gamma.rearrange("(c a) -> c a", a=1)).then_inc(par_in, 16)
                act.dma_start(bet[h * C:(h + 1) * C, :], beta.rearrange("(c a) -> c a", a=1)).then_inc(par_in, 16)
            act.dma_start(w_a[C:2 * C, :], W1[0:C, :]).then_inc(par_in, 16)
            act.dma_start(w2[:, :], W2).then_inc(par_in, 16)
            act.dma_start(b1c[:, :], b1.rearrange("(c a) -> c a", a=1)).then_inc(par_in, 16)
            act.dma_start(b2b[:, :], b2.rearrange("(a c) -> a c", a=1).to_broadcast([P, C])).then_inc(par_in, 16)
            act.sem_inc(acc_sb, 1)
            act.sem_inc(end_step, ND)
            act.sem_inc(y_out, CREDIT_DMA)
            act.wait_ge(step_ready, 1)
            act.activation(down[:, :], step[:, :], ACT.Relu, scale=-1.0, accum_out=order_col[:, :]).then_inc(order_ready, 1)
            act.wait_ge(xc_ready, 1)
            act.activation(xc[0:PN, :, :], xc[0:PN, :, :], ACT.Square).then_inc(sq_ready, 1)
            for b, t0, t1 in LAST_CUTS:
                act.wait_ge(last_ps, b + 1)
                act.activation(last_key[:, t0:t1, :], ps_last[b][:, 0:(t1 - t0) * NSB].rearrange("p (t s) -> p t s", s=NSB),
                               ACT.Copy).then_inc(last_ready, 1)
            act.wait_ge(std_in, 1)
            act.activation(bn[:, 2:3], bn[:, 1:2], ACT.Sqrt).then_inc(std_ready, 1)
            act.wait_ge(weights_ready, 1)
            act.wait_ge(src_ix_ready, TB)
            act.wait_ge(ones_ready, 4)
            act.wait_ge(flag_ready, 1)
            windowed = act.value_load(in_order[0:1, 0:1], min_val=0, max_val=1)
            with act.If(windowed == 1):
                with act.Fori(0, ITERS) as it:
                    base = it * IG
                    for k in range(IG + 2):
                        if k < IG:
                            act.wait_ge(feat_ps, base + (IG + k + 1))
                            if k >= 2:
                                act.wait_ge(hid_ps, base + (k - 1))
                            act.activation(feat[:, k % 2, :], ps_feat[:, k % 2, :], ACT.Copy).then_inc(feat_sb, 1)
                        j = k - 2
                        if 0 <= j < IG:
                            act.wait_ge(rows_ps, base + (j + 1))
                            if j >= 2:
                                act.wait_ge(acc_ps, base + (j - 1))
                            act.activation(rows[:, j % 2, :, 0:C], ps_rows[:, 0:TG * C].rearrange("p (t c) -> p t c", c=C),
                                           ACT.Copy).then_inc(rows_sb, 1)
                        if k < IG:
                            act.wait_ge(hid_ps, base + (k + 1))
                            if k >= 2:
                                act.wait_ge(msg_ps, base + (k - 1))
                            act.activation(hid[:, k % 2, :], ps_hid[:, k % 2, :], ACT.Relu,
                                           bias=bias1[:, :]).then_inc(hid_sb, 1)
                        if k in AT_ACC:
                            take_acc(it * 2 + AT_ACC.index(k))
                        if k in AT_STD:
                            deviation(it * 2 + AT_STD.index(k))
            with act.Else():
                act.wait_ge(g_dst_out, 16)
                with act.Fori(0, GT) as i:
                    act.wait_ge(g_merged, i * P + 1)
                    act.dma_start(pair_dst[:, :], dst_dram[bass.ds(i * P + GT0 * P, P)].rearrange("(p a) -> p a", a=1)).then_inc(g_dst_in, 16)
                    act.dma_start(dst_row[:, :], dst_dram[bass.ds(i * P + GT0 * P, P)].rearrange("(a e) -> a e", a=1)).then_inc(g_dst_in, 16)
                    act.wait_ge(g_feat_ps, i + 1)
                    act.activation(feat[:, 0, 0:P], ps_feat[:, 0, 0:P], ACT.Copy).then_inc(g_feat, 1)
                    act.wait_ge(g_hid_ps, i + 1)
                    act.activation(hid[:, 0, 0:P], ps_hid[:, 0, 0:P], ACT.Relu, bias=bias1[:, :]).then_inc(g_hid, 1)

                def node_block(b, first):
                    take_acc(b)
                    deviation(b)

                node_blocks(act, node_block)

        @block.vector
        def _(dve):
            done = [0]

            def chain(ins):
                done[0] += 1
                ins.then_inc(dve_step, 1)
                dve.wait_ge(dve_step, done[0])

            def centre(s, u, loads):
                n0 = s * ND + ND
                dve.wait_ge(acc_sb, s + 2)
                dve.scalar_tensor_tensor(res[:, :], b2b[:, :], acc[:, C:C1], acc[:, 0:C], ALU.mult, ALU.add).then_inc(end_step, 1)
                dve.wait_ge(xwin_in[u], loads * 16)
                dve.wait_ge(end_step, n0 + 1)
                dve.scalar_tensor_tensor(res[:, :], res[:, :], 0.0, xwin[u][:, :], ALU.max, ALU.add).then_inc(end_step, 1)
                dve.wait_ge(end_step, n0 + 2)
                dve.tensor_reduce(norm[:, 0:1], res[:, :], AX.X, ALU.add).then_inc(end_step, 1)
                dve.wait_ge(end_step, n0 + 3)
                dve.tensor_scalar(norm[:, 1:2], norm[:, 0:1], 1.0 / C, None, ALU.mult).then_inc(end_step, 1)
                dve.wait_ge(end_step, n0 + 4)
                dve.tensor_scalar(cen[:, :], res[:, :], norm[:, 1:2], None, ALU.subtract).then_inc(end_step, 1)

            def normalise(s):
                dve.wait_ge(end_std, s + 1)
                dve.reciprocal(norm[:, 4:5], norm[:, 3:4]).then_inc(end_step, 1)
                dve.wait_ge(y_out, s * 16 + CREDIT_DMA)
                dve.wait_ge(end_step, s * ND + 2 * ND)
                dve.tensor_scalar(y[:, :], cen[:, :], norm[:, 4:5], None, ALU.mult).then_inc(y_ready, 1)

            dve.wait_ge(src_first, 32 if PART else 16)
            dve.wait_ge(src_pad_ready, 1 + (FIRST > 0))
            dve.tensor_copy(src_f[:, 0, :], src_t[:, 0, :]).then_inc(src_f_ready, 1)
            dve.wait_ge(src_ps, 1)
            for u in range(2):
                dve.tensor_copy(ix[u][:, :], ps_src[0][:, u * ST:(u + 1) * ST]).then_inc(ix_first, 1)
            dve.memset(dst_r[:, SE + 1:SE + 2], N).then_inc(pads_ready, 1)
            dve.memset(dst_r[0:1, 0:1 + PAD], -1).then_inc(pads_ready, 1)
            dve.memset(first_dst[:, :], N - 1).then_inc(pads_ready, 1)
            dve.memset(runmax[:, 1, GE - 1:GE], SCALE)
            dve.memset(ones[:, :], 1.0).then_inc(ones_ready, 1)
            dve.memset(rows[:, :, :, C:C1], 1.0).then_inc(ones_ready, 1)
            dve.memset(eps_col[:, :], EPS).then_inc(ones_ready, 1)
            for t in SKIP:
                dve.memset(xs[:, t // TG, t % TG, :], 0.0).then_inc(skip_ready, 1)
            dve.memset(acc[:, :], 0.0).then_inc(ones_ready, 1)
            dve.sem_inc(g_merged, 1)
            dve.tensor_copy(src_ix[:, 0:P], ps_src[0]).then_inc(src_ix_ready, 1)
            dve.wait_ge(src_in, 16 * ((TILES // P > 1) + (TILES % P > 0)))
            dve.tensor_copy(src_f[:, 1:TB, :], src_t[:, 1:TB, :]).then_inc(src_f_ready, 1)
            for b in range(1, TB):
                dve.wait_ge(src_ps, b + 1)
                dve.tensor_copy(src_ix[:, b * P:(b + 1) * P], ps_src[b % 4]).then_inc(src_ix_ready, 1)
            dve.wait_ge(dst_in, 64 if SMID else 48)
            chain(dve.tensor_scalar(win_col[:, :], dst_r[:, 1:2], float(N - P), -1.0, ALU.min, ALU.add))
            chain(dve.memset(win_col[0:1, :], -1.0))
            dve.tensor_scalar(keys[:, :], dst_r[:, 0:SE + 1], win_col[:, :], SCALE, ALU.subtract, ALU.mult).then_inc(keys_ready, 1)
            dve.tensor_tensor(step[:, :], dst_r[:, 1:SE + 2], dst_r[:, 0:SE + 1], ALU.subtract).then_inc(step_ready, 1)
            dve.wait_ge(x_in, 16)
            dve.tensor_reduce(part[0:PN, :], xn[0:PN, :, :].rearrange("p t c -> p c t"), AX.X, ALU.add).then_inc(part_ready, 1)
            dve.wait_ge(win_in, 16)
            chain(dve.tensor_scalar(win0[:, :], first_dst[:, :], float(N - P), None, ALU.min))
            chain(dve.memset(win0[:, 0:1], 0))
            dve.memset(moved[:, 0:1], 0.0).then_inc(moved_ready, 1)
            dve.tensor_tensor(moved[:, 1:NSB], win0[:, 1:NSB], win0[:, 0:NSB - 1], ALU.subtract).then_inc(moved_ready, 1)
            chain(dve.tensor_tensor(win_step[:, :], first_dst[:, 1:NSB + 1], win0[:, 0:NSB], ALU.subtract))
            chain(dve.tensor_reduce(order[:, 0:1], win_step[:, :], AX.X, ALU.max))
            chain(dve.tensor_scalar(order[:, 1:2], order[:, 0:1], -1.0, float(P - 1), ALU.mult, ALU.add))
            dve.wait_ge(sum_ps, 1)
            chain(dve.tensor_scalar(mean_b[:, :], ps_sum, 1.0 / N, None, ALU.mult))
            dve.tensor_tensor(xc[0:PN, :, :], xn[0:PN, :, :],
                              mean_b[0:PN, :].rearrange("p (a c) -> p a c", a=1).to_broadcast([PN, TN, C]),
                              ALU.subtract).then_inc(xc_ready, 1)
            dve.wait_ge(order_ps, 1)
            chain(dve.tensor_scalar(order[:, 2:3], ps_order, -1.0, None, ALU.mult))
            chain(dve.tensor_tensor(order[:, 3:4], order[:, 1:2], order[:, 2:3], ALU.min))
            dve.tensor_scalar(in_order[:, :], order[:, 3:4], 0.0, None, ALU.is_ge).then_inc(flag_ready, 1)
            dve.wait_ge(consts_ready, 4)
            dve.tensor_scalar(slot_key[:, :], slot_col[:, :], SCALE, None, ALU.mult).then_inc(slot_keys_ready, 1)
            dve.tensor_scalar(slot_keys[:, :], slot_row[:, :], SCALE, None, ALU.mult).then_inc(slot_keys_ready, 1)
            dve.wait_ge(moved_ps, 1)
            dve.tensor_scalar(carry_col[:, :], ps_moved, -1.0, slot_col[:, :], ALU.mult, ALU.add).then_inc(carry_ready, 1)
            dve.wait_ge(step_ready, 1)
            dve.wait_ge(keys_ready, 1)
            dve.scalar_tensor_tensor(last_r[:, :], step[:, 1:SE + 1], 0.0, keys[:, 1:SE + 1], ALU.is_gt, ALU.mult).then_inc(last_r_ready, 1)
            dve.wait_ge(sq_ready, 1)
            dve.tensor_reduce(part_sq[0:PN, :], xc[0:PN, :, :].rearrange("p t c -> p c t"), AX.X, ALU.add).then_inc(part_ready, 1)
            dve.wait_ge(var_ps, 1)
            dve.tensor_scalar(bn[:, 1:2], ps_var[:, 0:1], 1.0 / N, EPS, ALU.mult, ALU.add).then_inc(std_in, 1)
            chain(dve.tensor_scalar(bn[:, 0:1], ps_var[:, 1:2], 1.0 / N, None, ALU.mult))
            dve.wait_ge(std_ready, 1)
            dve.wait_ge(par_in, 160)
            chain(dve.reciprocal(bn[:, 3:4], bn[:, 2:3]))
            chain(dve.tensor_tensor(bn[:, 4:5], bn[:, 3:4], gam[:, :], ALU.mult))
            chain(dve.tensor_tensor(bn[:, 3:4], bn[:, 0:1], bn[:, 4:5], ALU.mult))
            chain(dve.tensor_tensor(bn[:, 5:6], bet[:, :], bn[:, 3:4], ALU.subtract))
            chain(dve.tensor_tensor(w_raw[C:2 * C, :], w_a[C:2 * C, :], w_raw[C:2 * C, :], ALU.subtract))
            dve.tensor_scalar(w_cat[:, :], w_raw[:, :], bn[:, 4:5], None, ALU.mult).then_inc(fold_ready, 1)
            dve.wait_ge(bias_ps, 1)
            dve.tensor_tensor(bias1[:, :], ps_bias, b1c[:, :], ALU.add).then_inc(weights_ready, 1)
            dve.wait_ge(slot_keys_ready, 2)
            dve.wait_ge(carry_ready, 1)
            dve.wait_ge(last_ready, len(LAST_CUTS))
            dve.wait_ge(flag_ready, 1)
            windowed = dve.value_load(in_order[0:1, 0:1], min_val=0, max_val=1)
            with dve.If(windowed == 1):
                with dve.Fori(0, ITERS) as it:
                    base = it * IG
                    for k in range(IG + 2):
                        if k < IG:
                            u, g = divmod(k, SG)
                            e0 = KB0 + g * GE
                            if g == 0:
                                n0 = u * 4
                                dve.wait_ge(xwin_in[u], it * 16 + 16)
                                dve.tensor_copy(xw[u][:, 0, :], xwin[u][:, :]).then_inc(split_step, 1)
                                dve.wait_ge(split_step, it * 8 + (n0 + 1))
                                dve.tensor_tensor(xw_rest[:, :], xwin[u][:, :], xw[u][:, 0, :], ALU.subtract).then_inc(split_step, 1)
                                dve.wait_ge(split_step, it * 8 + (n0 + 2))
                                dve.tensor_copy(xw[u][:, 1, :], xw_rest[:, :]).then_inc(split_step, 1)
                                dve.wait_ge(split_step, it * 8 + (n0 + 3))
                                dve.tensor_tensor(xw[u][:, 2, :], xw_rest[:, :], xw[u][:, 1, :], ALU.subtract).then_inc(split_step, 1)
                                dve.wait_ge(key_in[u], it * 16 + 16)
                            if k >= 2:
                                dve.wait_ge(feat_ps, base + (IG + k - 1))
                            dve.tensor_scalar(onehot[:, k % 2, :], kb[u][:, e0:e0 + GE], slot_key[:, :], None,
                                              ALU.is_equal).then_inc(onehot_ready, 1)
                            dve.tensor_tensor(reset[:, g, :], kb[u][0:C, e0:e0 + GE], kb[u][0:C, e0 - 1:e0 - 1 + GE],
                                              ALU.subtract).then_inc(reset_ready, 1)
                        j = k - 2
                        if 0 <= j < IG:
                            u, g = divmod(j, SG)
                            if j >= 2:
                                dve.wait_ge(acc_ps, base + (j - 1))
                            if g == 0:
                                dve.tensor_tensor(shift[:, :], slot_row[:, :], carry_col[:, bass.ds(it * 2 + u, 1)].to_broadcast([P, P]),
                                                  ALU.is_equal).then_inc(shift_ready, 1)
                            dve.tensor_tensor(pick[:, j % 2, :, :],
                                              slot_keys[:, :].rearrange("p (a n) -> p a n", a=1).to_broadcast([P, TG, P]),
                                              last_key[:, g * TG:(g + 1) * TG, bass.ds(it * 2 + u, 1)].to_broadcast([P, TG, P]),
                                              ALU.is_equal).then_inc(pick_ready, 1)
                            dve.wait_ge(msg_ps, base + (j + 1))
                            dve.wait_ge(reset_ready, base + (j + 1))
                            if j >= 2:
                                dve.wait_ge(rows_ps, base + (j - 1))
                            if j > 0:
                                dve.wait_ge(run_ready, base + j)
                            dve.tensor_tensor_scan(runmax[:, j % 2, :], reset[:, j % SG, :], ps_msg[0:C, j % 2, :],
                                                   runmax[:, (j + 1) % 2, GE - 1:GE], ALU.add, ALU.max).then_inc(run_ready, 1)
                        if k in AT_CENTRE:
                            u = AT_CENTRE.index(k)
                            centre(it * 2 + u, u, it + 1)
                        if k in AT_NORM:
                            normalise(it * 2 + AT_NORM.index(k))
            with dve.Else():
                dve.memset(best[0:C, :], SCALE).then_inc(g_msg, 1)
                dve.memset(best[C:C1, :], 0.0).then_inc(g_msg, 1)
                dve.memset(msg[C:C1, :], 1.0).then_inc(g_msg, 1)
                with dve.Fori(0, GT) as i:
                    dve.wait_ge(g_dst_in, i * 32 + 32)
                    dve.tensor_scalar(col_row[:, :], dst_row[:, :], 1.0, None, ALU.add).then_inc(g_col, 1)
                    dve.wait_ge(g_msg_ps, i + 1)
                    dve.wait_ge(g_col, i + 1)
                    dve.tensor_copy(msg[0:C, :], ps_msg[0:C, 0, 0:P]).then_inc(g_msg, 1)
                    with dve.Fori(0, P) as e:
                        node = dve.value_load(col_row[0:1, bass.ds(e, 1)], min_val=0, max_val=N)
                        dve.wait_ge(g_msg, i + 4)
                        dve.wait_ge(g_merged, i * P + e + 1)
                        dve.tensor_tensor(best[:, bass.ds(node, 1)], best[:, bass.ds(node, 1)], msg[:, bass.ds(e, 1)],
                                          ALU.max).then_inc(g_merged, 1)

                def node_block(b, first):
                    dve.wait_ge(g_merged, GT * P + 1)
                    dve.tensor_copy(msg[:, :], best[:, bass.ds(first + 1, P)]).then_inc(g_block, 1)
                    centre(b, 0, b + 1)
                    normalise(b)

                node_blocks(dve, node_block)

        @block.tensor
        def _(pe):
            pe.sem_inc(feat_ps, IG)
            pe.wait_ge(consts_ready, 4)
            for b in range(TB):
                pe.wait_ge(src_f_ready, 1 if b == 0 else 2)
                if b >= 4:
                    pe.wait_ge(src_ix_ready, b - 3)
                pe.transpose(ps_src[b % 4], src_f[:, b, :], ident[:, :]).then_inc(src_ps, 1)
            pe.wait_ge(ones_ready, 1)
            pe.wait_ge(part_ready, 1)
            pe.matmul(ps_sum, ones[0:PN, :], part[0:PN, :], start=True, stop=True).then_inc(sum_ps, 1)
            pe.wait_ge(order_ready, 1)
            pe.matmul(ps_order, order_col[:, :], ones[0:NSB, 0:1], start=True, stop=True).then_inc(order_ps, 1)
            pe.wait_ge(moved_ready, 2)
            pe.matmul(ps_moved, ones[0:1, :], moved[:, :], start=True, stop=True).then_inc(moved_ps, 1)
            pe.wait_ge(src_ix_ready, TB)
            pe.wait_ge(last_r_ready, 1)
            for b, t0, t1 in LAST_CUTS:
                for t in range(t0, t1):
                    last = pe.transpose(ps_last[b][:, (t - t0) * NSB:(t - t0 + 1) * NSB], last_r[:, t * P:(t + 1) * P],
                                        ident[0:NSB, 0:NSB])
                last.then_inc(last_ps, 1)
            pe.wait_ge(part_ready, 2)
            for col, of in ((0, part_sq), (1, part)):
                for h in range(2):
                    last = pe.matmul(ps_var[h * C:(h + 1) * C, col:col + 1], of[0:PN, :], ones[0:PN, 0:1], start=True, stop=True)
            last.then_inc(var_ps, 1)
            pe.wait_ge(carry_ready, 1)
            pe.wait_ge(fold_ready, 1)
            pe.matmul(ps_bias, w_raw[:, :], bn[:, 5:6], start=True, stop=True).then_inc(bias_ps, 1)
            pe.wait_ge(weights_ready, 1)
            pe.wait_ge(last_ready, len(LAST_CUTS))
            if SKIP:
                pe.wait_ge(skip_ready, len(SKIP))
            pe.wait_ge(flag_ready, 1)
            windowed = pe.value_load(in_order[0:1, 0:1], min_val=0, max_val=1)
            with pe.If(windowed == 1):
                with pe.Fori(0, ITERS) as it:
                    base = it * IG
                    for k in range(IG + 2):
                        if k < IG:
                            u, g = divmod(k, SG)
                            if k >= 2:
                                pe.wait_ge(feat_sb, base + (k - 1))
                            pe.wait_ge(rows_in[k], it * (16 * TG) + ROWS0[k])
                            if g == 0:
                                pe.wait_ge(split_step, it * 8 + 4 * (u + 1))
                            pe.wait_ge(onehot_ready, base + (k + 1))
                            for w in range(3):
                                pe.matmul(ps_feat[C:2 * C, k % 2, :], xw[u][:, w, :], onehot[:, k % 2, :], start=(w == 0), stop=(w == 2))
                            for t in range(TG):
                                last = pe.transpose(ps_feat[0:C, k % 2, t * P:(t + 1) * P], xs[:, k, t, :], ident[:, :])
                            last.then_inc(feat_ps, 1)
                        j = k - 2
                        if 0 <= j < IG:
                            pe.wait_ge(consts_ready, 4)
                            pe.wait_ge(run_ready, base + (j + 1))
                            for t in range(TG):
                                last = pe.transpose(ps_rows[:, t * C:(t + 1) * C], runmax[:, j % 2, t * P:(t + 1) * P], ident[0:C, 0:C])
                            last.then_inc(rows_ps, 1)
                        j = k - 1
                        if 0 <= j < IG:
                            pe.wait_ge(hid_sb, base + (j + 1))
                            if j >= 2:
                                pe.wait_ge(run_ready, base + (j - 1))
                            pe.matmul(ps_msg[0:C, j % 2, :], w2[:, :], hid[:, j % 2, :], start=True, stop=True).then_inc(msg_ps, 1)
                        if k < IG:
                            pe.wait_ge(feat_sb, base + (k + 1))
                            if k >= 2:
                                pe.wait_ge(hid_sb, base + (k - 1))
                            pe.matmul(ps_hid[:, k % 2, :], w_cat[:, :], feat[:, k % 2, :], start=True, stop=True).then_inc(hid_ps, 1)
                        j = k - 2
                        if 0 <= j < IG:
                            u, g = divmod(j, SG)
                            pe.wait_ge(rows_sb, base + (j + 1))
                            pe.wait_ge(pick_ready, base + (j + 1))
                            if g == 0:
                                pe.wait_ge(acc_sb, it * 2 + (u + 1))
                                pe.wait_ge(shift_ready, it * 2 + (u + 1))
                                pe.matmul(ps_acc[:, 0:C1], shift[:, :], acc[:, :], start=True, stop=False)
                            for t in range(TG):
                                last = pe.matmul(ps_acc[:, 0:C1], pick[:, j % 2, t, :], rows[:, j % 2, t, :],
                                                 start=False, stop=(g == SG - 1 and t == TG - 1))
                            last.then_inc(acc_ps, 1)
            with pe.Else():
                with pe.Fori(0, GT) as i:
                    pe.wait_ge(g_pair_in, i * 32 + 32)
                    pe.transpose(ps_feat[:, 0, 0:P], pair[:, :, :].rearrange("p s c -> p (s c)"), ident[:, :]).then_inc(g_feat_ps, 1)
                    pe.wait_ge(g_feat, i + 1)
                    pe.matmul(ps_hid[:, 0, 0:P], w_cat[:, :], feat[:, 0, 0:P], start=True, stop=True).then_inc(g_hid_ps, 1)
                    pe.wait_ge(g_hid, i + 1)
                    pe.matmul(ps_msg[0:C, 0, 0:P], w2[:, :], hid[:, 0, 0:P], start=True, stop=True).then_inc(g_msg_ps, 1)

                def node_block(b, first):
                    pe.wait_ge(consts_ready, 4)
                    pe.wait_ge(acc_sb, b + 1)
                    pe.wait_ge(g_block, b + 1)
                    pe.transpose(ps_acc[:, 0:C1], msg[:, :], ident[0:C1, 0:C1]).then_inc(acc_ps, SG)

                node_blocks(pe, node_block)



_INS = ["x", "src", "dst", "L0_gnn_gamma", "L0_gnn_beta", "L0_gnn_W1", "L0_gnn_b1", "L0_gnn_W2", "L0_gnn_b2"]


def kernel(**inputs):
    import concourse.bacc as bacc
    from concourse.bass_utils import run_bass_kernel_spmd as run

    nc = bacc.Bacc("TRN2", target_bir_lowering=False, num_devices=1)
    arrays, args = {}, []
    for name in _INS:
        a = np.ascontiguousarray(inputs[name])
        arrays[f"in_{name}"] = a
        args.append(nc.dram_tensor(f"in_{name}", a.shape, mybir.dt.from_np(a.dtype), kind="ExternalInput").ap())
    out = nc.dram_tensor("out_0", inputs["x"].shape, mybir.dt.float32, kind="ExternalOutput").ap()
    edge_conv_program(nc, *args, out)
    r = run(nc, [arrays], core_ids=[0])
    return r.results[0]["out_0"]
```
